# Optimizing a Trainium2 kernel written in Bass

```python
import numpy as np
import jax
import jax.numpy as jnp

def _softmax(x, axis=-1):
    return jax.nn.softmax(x, axis=axis)

def _gelu(x):
    return jax.nn.gelu(x, approximate=True)

def _silu(x):
    return jax.nn.silu(x)

def _sigmoid(x):
    return jax.nn.sigmoid(x)

def _layernorm(x, axis=-1, eps=1e-05):
    m = jnp.mean(x, axis=axis, keepdims=True)
    v = jnp.var(x, axis=axis, keepdims=True)
    return (x - m) / jnp.sqrt(v + eps)

def _scatter_add(tgt, idx, src, axis=0):
    return tgt.at[idx].add(src)

def _segment_sum(src, seg, n):
    return jax.ops.segment_sum(src, seg, n)
kernel_name = 'mk_gnn_ffn_d1_gnn_r32_0952ef'

def setup_inputs(seed: int=0):
    np.random.seed(seed)
    _w = jnp.asarray

    def _rec_inputs():
        import jax
        import jax.numpy as jnp
        _gk = jax.random.key(seed)
        x = -6.985e-05 + 0.9998 * jax.random.normal(jax.random.fold_in(_gk, 1), (10000, 512), jnp.float32)
        src = jax.random.randint(jax.random.fold_in(_gk, 2), (10000,), 0, 10000, jnp.int32)
        dst = jnp.minimum((10000 * jax.random.uniform(jax.random.fold_in(_gk, 3), (10000,)) ** 2.0).astype(jnp.int32), 9999)
        _o = jnp.argsort(dst, stable=True)
        src = src[_o]
        dst = dst[_o]
        return (x, src, dst)
    x, src, dst = _rec_inputs()

    def _L0_gnn_setup():
        import jax, jax.numpy as jnp
        import numpy as np
        B = 32
        MAXN = 64
        HEADS = 8
        DH = 64
        M = 256
        D = 512
        EPS = 1e-05
        KEPS = 1e-06

        def _batchnorm(x, g, b):
            mu = jnp.mean(x, axis=0)
            var = jnp.mean((x - mu) ** 2, axis=0)
            return (x - mu) * jax.lax.rsqrt(var + EPS) * g + b

        def _forward(x, batch, edge_index, norm1_g, norm1_b, norm2_g, norm2_b, W_conv, b_conv, Wq, Wk, Wv, Wo, proj):
            N = x.shape[0]
            E = edge_index.shape[1]
            h = x
            xn = _batchnorm(x, norm1_g, norm1_b)
            msg = xn[edge_index[0]]
            agg = jax.ops.segment_sum(msg, edge_index[1], num_segments=N)
            deg = jax.ops.segment_sum(jnp.ones((E,), x.dtype), edge_index[1], num_segments=N)
            agg = agg / jnp.maximum(deg, 1.0)[:, None]
            conv_out = jax.nn.relu(agg @ W_conv + b_conv)
            counts = jax.ops.segment_sum(jnp.ones((N,), jnp.int32), batch, num_segments=B)
            offsets = jnp.concatenate([jnp.zeros((1,), jnp.int32), jnp.cumsum(counts)[:-1]])
            pos = jnp.arange(N, dtype=jnp.int32) - offsets[batch]
            h_dense = jnp.zeros((B, MAXN, D), x.dtype).at[batch, pos].set(h)
            mask = jnp.zeros((B, MAXN), bool).at[batch, pos].set(True)

            def heads(t, W):
                return (t @ W).reshape(B, MAXN, HEADS, DH).transpose(0, 2, 1, 3)
            q, k, v = (heads(h_dense, Wq), heads(h_dense, Wk), heads(h_dense, Wv))
            scale = DH ** (-0.25)

            def phi(t, is_query):
                t = t * scale
                u = jnp.einsum('bhnd,md->bhnm', t, proj)
                diag = 0.5 * jnp.sum(t * t, axis=-1, keepdims=True)
                if is_query:
                    m_ = jnp.max(u, axis=-1, keepdims=True)
                else:
                    m_ = jnp.max(u, axis=(-2, -1), keepdims=True)
                return jnp.exp(u - diag - jax.lax.stop_gradient(m_)) / np.sqrt(M) + KEPS
            qf = phi(q, True)
            kf = phi(k, False) * mask[:, None, :, None]
            vm = v * mask[:, None, :, None]
            kv = jnp.einsum('bhnm,bhnd->bhmd', kf, vm)
            z = 1.0 / (jnp.einsum('bhnm,bhm->bhn', qf, kf.sum(axis=2)) + KEPS)
            attn = jnp.einsum('bhnm,bhmd->bhnd', qf, kv) * z[..., None]
            attn = attn.transpose(0, 2, 1, 3).reshape(B, MAXN, D) @ Wo
            h_attn = attn[batch, pos]
            return _batchnorm(conv_out + h_attn + h, norm2_g, norm2_b)
        key = jax.random.key(seed)
        ks = jax.random.split(key, 10)
        sizes = 1024 + np.arange(B) * 131 % 1025
        N = int(sizes.sum())
        E = N * 8
        batch = jnp.asarray(np.repeat(np.arange(B), sizes), dtype=jnp.int32)
        edge_index = jax.random.randint(ks[0], (2, E), 0, N, dtype=jnp.int32)
        s = 1.0 / np.sqrt(D)
        return {'x': jax.random.normal(ks[1], (N, D), jnp.float32), 'batch': batch, 'edge_index': edge_index, 'norm1_g': jnp.ones((D,), jnp.float32), 'norm1_b': jnp.zeros((D,), jnp.float32), 'norm2_g': jnp.ones((D,), jnp.float32), 'norm2_b': jnp.zeros((D,), jnp.float32), 'W_conv': jax.random.normal(ks[2], (D, D), jnp.float32) * s, 'b_conv': jnp.zeros((D,), jnp.float32), 'Wq': jax.random.normal(ks[3], (D, D), jnp.float32) * s, 'Wk': jax.random.normal(ks[4], (D, D), jnp.float32) * s, 'Wv': jax.random.normal(ks[5], (D, D), jnp.float32) * s, 'Wo': jax.random.normal(ks[6], (D, D), jnp.float32) * s, 'proj': jax.random.normal(ks[7], (M, DH), jnp.float32)}
    _L0_gnn_all = _L0_gnn_setup()
    _L0_gnn_in = {k: v for k, v in _L0_gnn_all.items() if k in ('norm1_g', 'norm1_b', 'norm2_g', 'norm2_b', 'W_conv', 'b_conv', 'Wq', 'Wk', 'Wv', 'Wo', 'proj')}
    del _L0_gnn_all

    def _L0_ffn_setup():
        import jax, jax.numpy as jnp
        import numpy as np
        S, B, D, F, E, K = (1024, 2, 512, 64, 8, 2)
        key = jax.random.key(seed)
        ks = jax.random.split(key, 12)
        s = lambda *sh: 1.0 / np.sqrt(sh[0])
        inp = {'x': jax.random.normal(ks[0], (S, B, D), dtype=jnp.float32), 'Wg': jax.random.normal(ks[1], (D, E), dtype=jnp.float32) * s(D), 'bg': jnp.zeros((E,), dtype=jnp.float32), 'W1': jax.random.normal(ks[2], (E, D, F), dtype=jnp.float32) * s(D), 'b1': jnp.zeros((E, F), dtype=jnp.float32), 'W2': jax.random.normal(ks[3], (E, F, D), dtype=jnp.float32) * s(F), 'b2': jnp.zeros((E, D), dtype=jnp.float32), 'Ws1': jax.random.normal(ks[4], (D, F), dtype=jnp.float32) * s(D), 'bs1': jnp.zeros((F,), dtype=jnp.float32), 'Ws2': jax.random.normal(ks[5], (F, D), dtype=jnp.float32) * s(F), 'bs2': jnp.zeros((D,), dtype=jnp.float32)}
        return inp
    _L0_ffn_all = _L0_ffn_setup()
    _L0_ffn_in = {k: v for k, v in _L0_ffn_all.items() if k in ('Wg', 'bg', 'W1', 'b1', 'W2', 'b2', 'Ws1', 'bs1', 'Ws2', 'bs2')}
    del _L0_ffn_all
    return {'x': x, 'src': src, 'dst': dst, 'L0_gnn_norm1_g': _L0_gnn_in['norm1_g'], 'L0_gnn_norm1_b': _L0_gnn_in['norm1_b'], 'L0_gnn_norm2_g': _L0_gnn_in['norm2_g'], 'L0_gnn_norm2_b': _L0_gnn_in['norm2_b'], 'L0_gnn_W_conv': _L0_gnn_in['W_conv'], 'L0_gnn_b_conv': _L0_gnn_in['b_conv'], 'L0_gnn_Wq': _L0_gnn_in['Wq'], 'L0_gnn_Wk': _L0_gnn_in['Wk'], 'L0_gnn_Wv': _L0_gnn_in['Wv'], 'L0_gnn_Wo': _L0_gnn_in['Wo'], 'L0_gnn_proj': _L0_gnn_in['proj'], 'L0_ffn_Wg': _L0_ffn_in['Wg'], 'L0_ffn_bg': _L0_ffn_in['bg'], 'L0_ffn_W1': _L0_ffn_in['W1'], 'L0_ffn_b1': _L0_ffn_in['b1'], 'L0_ffn_W2': _L0_ffn_in['W2'], 'L0_ffn_b2': _L0_ffn_in['b2'], 'L0_ffn_Ws1': _L0_ffn_in['Ws1'], 'L0_ffn_bs1': _L0_ffn_in['bs1'], 'L0_ffn_Ws2': _L0_ffn_in['Ws2'], 'L0_ffn_bs2': _L0_ffn_in['bs2']}

def reference(x, src, dst, L0_gnn_norm1_g, L0_gnn_norm1_b, L0_gnn_norm2_g, L0_gnn_norm2_b, L0_gnn_W_conv, L0_gnn_b_conv, L0_gnn_Wq, L0_gnn_Wk, L0_gnn_Wv, L0_gnn_Wo, L0_gnn_proj, L0_ffn_Wg, L0_ffn_bg, L0_ffn_W1, L0_ffn_b1, L0_ffn_W2, L0_ffn_b2, L0_ffn_Ws1, L0_ffn_bs1, L0_ffn_Ws2, L0_ffn_bs2):
    import jax
    import jax.numpy as jnp

    def _L0_gnn_ref(x, batch, edge_index, norm1_g, norm1_b, norm2_g, norm2_b, W_conv, b_conv, Wq, Wk, Wv, Wo, proj):
        import jax, jax.numpy as jnp
        import numpy as np
        B = 32
        MAXN = 64
        HEADS = 8
        DH = 64
        M = 256
        D = 512
        EPS = 1e-05
        KEPS = 1e-06

        def _batchnorm(x, g, b):
            mu = jnp.mean(x, axis=0)
            var = jnp.mean((x - mu) ** 2, axis=0)
            return (x - mu) * jax.lax.rsqrt(var + EPS) * g + b

        def _forward(x, batch, edge_index, norm1_g, norm1_b, norm2_g, norm2_b, W_conv, b_conv, Wq, Wk, Wv, Wo, proj):
            N = x.shape[0]
            E = edge_index.shape[1]
            h = x
            xn = _batchnorm(x, norm1_g, norm1_b)
            msg = xn[edge_index[0]]
            agg = jax.ops.segment_sum(msg, edge_index[1], num_segments=N)
            deg = jax.ops.segment_sum(jnp.ones((E,), x.dtype), edge_index[1], num_segments=N)
            agg = agg / jnp.maximum(deg, 1.0)[:, None]
            conv_out = jax.nn.relu(agg @ W_conv + b_conv)
            counts = jax.ops.segment_sum(jnp.ones((N,), jnp.int32), batch, num_segments=B)
            offsets = jnp.concatenate([jnp.zeros((1,), jnp.int32), jnp.cumsum(counts)[:-1]])
            pos = jnp.arange(N, dtype=jnp.int32) - offsets[batch]
            h_dense = jnp.zeros((B, MAXN, D), x.dtype).at[batch, pos].set(h)
            mask = jnp.zeros((B, MAXN), bool).at[batch, pos].set(True)

            def heads(t, W):
                return (t @ W).reshape(B, MAXN, HEADS, DH).transpose(0, 2, 1, 3)
            q, k, v = (heads(h_dense, Wq), heads(h_dense, Wk), heads(h_dense, Wv))
            scale = DH ** (-0.25)

            def phi(t, is_query):
                t = t * scale
                u = jnp.einsum('bhnd,md->bhnm', t, proj)
                diag = 0.5 * jnp.sum(t * t, axis=-1, keepdims=True)
                if is_query:
                    m_ = jnp.max(u, axis=-1, keepdims=True)
                else:
                    m_ = jnp.max(u, axis=(-2, -1), keepdims=True)
                return jnp.exp(u - diag - jax.lax.stop_gradient(m_)) / np.sqrt(M) + KEPS
            qf = phi(q, True)
            kf = phi(k, False) * mask[:, None, :, None]
            vm = v * mask[:, None, :, None]
            kv = jnp.einsum('bhnm,bhnd->bhmd', kf, vm)
            z = 1.0 / (jnp.einsum('bhnm,bhm->bhn', qf, kf.sum(axis=2)) + KEPS)
            attn = jnp.einsum('bhnm,bhmd->bhnd', qf, kv) * z[..., None]
            attn = attn.transpose(0, 2, 1, 3).reshape(B, MAXN, D) @ Wo
            h_attn = attn[batch, pos]
            return _batchnorm(conv_out + h_attn + h, norm2_g, norm2_b)
        return _forward(x, batch, edge_index, norm1_g, norm1_b, norm2_g, norm2_b, W_conv, b_conv, Wq, Wk, Wv, Wo, proj)

    def _L0_ffn_ref(x, Wg, bg, W1, b1, W2, b2, Ws1, bs1, Ws2, bs2):
        import jax, jax.numpy as jnp
        import numpy as np
        S, B, D, F, E, K = (1024, 2, 512, 64, 8, 2)
        gate_logits = jnp.einsum('sbd,de->sbe', x, Wg) + bg
        weights, selected = jax.lax.top_k(gate_logits, K)
        weights = jax.nn.softmax(weights.astype(jnp.float32), axis=-1)
        onehot = jax.nn.one_hot(selected, E, dtype=weights.dtype)
        comb = jnp.einsum('sbk,sbke->sbe', weights, onehot)
        h = jax.nn.relu(jnp.einsum('sbd,edf->sbef', x, W1) + b1)
        y = jnp.einsum('sbef,efd->sbed', h, W2) + b2
        out = jnp.einsum('sbe,sbed->sbd', comb, y)
        hs = jax.nn.relu(jnp.einsum('sbd,df->sbf', x, Ws1) + bs1)
        shared = jnp.einsum('sbf,fd->sbd', hs, Ws2) + bs2
        out = out + 1.0 / K * shared
        return out
    edge_index = jnp.stack([src, dst])
    batch0 = jnp.zeros((10000,), jnp.int32)
    x = x + _L0_gnn_ref(_layernorm(x, axis=-1), batch0, edge_index, L0_gnn_norm1_g, L0_gnn_norm1_b, L0_gnn_norm2_g, L0_gnn_norm2_b, L0_gnn_W_conv, L0_gnn_b_conv, L0_gnn_Wq, L0_gnn_Wk, L0_gnn_Wv, L0_gnn_Wo, L0_gnn_proj)
    x = x + _L0_ffn_ref(_layernorm(x, axis=-1)[None], L0_ffn_Wg, L0_ffn_bg, L0_ffn_W1, L0_ffn_b1, L0_ffn_W2, L0_ffn_b2, L0_ffn_Ws1, L0_ffn_bs1, L0_ffn_Ws2, L0_ffn_bs2)[0]
    return x

_drawn_inputs = setup_inputs


def setup_inputs(seed=0):
    import zlib

    import numpy as np

    out = dict(_drawn_inputs(seed))
    spreads = {'L0_gnn_norm1_g': (1.0, 0.2),
     'L0_gnn_norm1_b': (0.0, 0.1),
     'L0_gnn_norm2_g': (1.0, 0.2),
     'L0_gnn_norm2_b': (0.0, 0.1),
     'L0_gnn_b_conv': (0.0, 0.1),
     'L0_ffn_bg': (0.0, 0.1),
     'L0_ffn_b1': (0.0, 0.322),
     'L0_ffn_b2': (0.0, 0.1),
     'L0_ffn_bs1': (0.0, 0.441),
     'L0_ffn_bs2': (0.0, 0.327)}
    factors = {'L0_gnn_Wq': 8.0, 'L0_gnn_Wk': 8.0, 'L0_gnn_Wv': 8.0, 'L0_gnn_Wo': 8.0, 'L0_gnn_proj': 8.0}
    for name, (base, spread) in spreads.items():
        noise = np.random.default_rng([zlib.crc32(name.encode()), seed]).standard_normal(out[name].shape)
        drawn = base * np.exp(spread * noise) if base else spread * noise
        out[name] = jnp.asarray(drawn.astype(out[name].dtype))
    for name, factor in factors.items():
        out[name] = (out[name] * factor).astype(out[name].dtype)
    return out
```

```python
from contextlib import ExitStack

import concourse.bass as bass
from concourse import mybir

F32 = mybir.dt.float32
F32R = mybir.dt.float32r
I32 = mybir.dt.int32
U32 = mybir.dt.uint32
ALU = mybir.AluOpType
ACT = mybir.ActivationFunctionType
AX_X = mybir.AxisListType.X
RMAX = bass.bass_isa.ReduceOp.max

P = 128
LN_EPS = 1e-5
BN_EPS = 1e-5
KEPS = 1e-6


class Sizes:
    def __init__(self, t):
        self.N, self.D = t["x"].shape
        self.E = t["src"].shape[0]
        self.DC = self.D // P
        self.M, self.DH = t["L0_gnn_proj"].shape
        self.H = self.D // self.DH
        self.NE, _, self.F = t["L0_ffn_W1"].shape
        self.HC = self.NE * self.F // P
        self.SEQ = 64
        self.FULL, self.REST = divmod(self.N, P)
        self.EF, self.ER = divmod(self.E, P)
        self.STEPS = -(-self.E // (2 * P))
        self.ET = 2 * self.STEPS
        self.DUMP = self.N
        self.PAD = self.N + 2 * P
        self.ZT = -(-(self.PAD + 1) // P)
        self.RW = self.D + 4
        self.GT = 4
        self.GN = self.GT * P
        self.NG = -(-self.N // self.GN)
        self.LAST = self.N - (self.NG - 1) * self.GN
        self.LAST_T = -(-self.LAST // P)
        assert self.D == 512 and self.E == self.N and self.M == 256 and self.DH == self.F == 64
        assert self.STEPS % 2 == 0 and self.NG % 2 == 0 and self.NE == 8
        assert 0 < self.REST < P and self.FULL == 2 * (self.STEPS - 1) and self.LAST % P == self.REST


class Order:

    def __init__(self, eng, sem, base=0):
        self.eng, self.sem, self.base, self.n = eng, sem, base, 0

    def count(self, ins):
        ins.then_inc(self.sem, 1)
        self.n += 1

    def then(self, ins, before=None):
        self.count(ins)
        if before is not None:
            in_register(self.eng, self.base + self.n)
            self.eng.wait_ge(*before)
        self.eng.wait_ge(self.sem, self.base + self.n)


def wait_unless_first(eng, sem, value):
    if not isinstance(value, int) or value > 0:
        eng.wait_ge(sem, value)


def in_register(eng, value):
    if not isinstance(value, int):
        eng.compute_val(value)
    return value


def gnn_moe_kernel(nc, t, out):
    z = Sizes(t)
    gsum = nc.dram_tensor("gsum", [z.ZT * P, z.RW], F32, kind="Internal").ap()
    zbuf = nc.dram_tensor("zbuf", [z.D, z.NG * z.GN], F32, kind="Internal").ap()
    with ExitStack() as ctx:
        def sb(name, shape, dt=F32):
            return ctx.enter_context(nc.sbuf_tensor(name, shape, dt))

        bank = [ctx.enter_context(nc.psum_tensor(f"bank{i}", [P, 512], F32)) for i in range(8)]
        ident = sb("ident", [P, P])
        node_affine = sb("node_affine", [P, z.ET, 2])
        attnT = sb("attnT", [P, z.DC, z.SEQ])
        bn1 = sb("bn1", [P, 2, z.DC])
        bn2 = sb("bn2", [P, 2, z.DC])
        with ExitStack() as scope:
            edges_and_statistics(nc, scope, z, t, bank, ident, node_affine, attnT, bn1, gsum)
        with ExitStack() as scope:
            convolution(nc, scope, z, t, bank, ident, node_affine, attnT, bn1, bn2, gsum, zbuf)
        with ExitStack() as scope:
            experts(nc, scope, z, t, bank, ident, bn2, zbuf, out)


def edges_and_statistics(nc, scope, z, t, bank, ident, node_affine, attnT, bn1, gsum):
    def sb(name, shape, dt=F32):
        return scope.enter_context(nc.sbuf_tensor(name, shape, dt))

    def sem(name):
        return scope.enter_context(nc.semaphore(name))

    N, D, E, DC, M, DH, H, SEQ = z.N, z.D, z.E, z.DC, z.M, z.DH, z.H, z.SEQ
    STEPS, ET, EF, ER, RW = z.STEPS, z.ET, z.EF, z.ER, z.RW
    MC = M // P
    FOURS = STEPS // 4
    SCALE = float(DH) ** -0.25
    ZEROED = 16 * STEPS
    ZEROED_LAST = z.ZT - 2 * (STEPS - 1)
    x, src, dst = t["x"], t["src"], t["dst"]

    dst_row = sb("dst_row", [P, ET * P], I32)
    edge_rows = sb("edge_rows", [ET, 2, P], I32)
    edge_rows_f = sb("edge_rows_f", [ET, 2, P])
    src_col = sb("src_col", [P, ET + 8], I32)
    dst_col = sb("dst_col", [P, ET])
    earlier = sb("earlier", [P, 2, 2 * P])
    dump_i = sb("dump_i", [P, 2], I32)
    dump_row = sb("dump_row", [P, 2])
    ones = sb("ones", [P, 1])
    neg_half = sb("neg_half", [P, 4])
    zeros = sb("zeros", [P, ZEROED_LAST * RW])
    gather_at = sb("gather_at", [P, 4, 2], I32)
    scatter_at = sb("scatter_at", [P, 4, 2], I32)
    edge_x = sb("edge_x", [P, 4, 2, D])
    edge_stats = sb("edge_stats", [P, 2, 6])
    edge_mv = sb("edge_mv", [P, 2, 2, 2])
    edge_affine = sb("edge_affine", [P, 2, 2, 2])
    edge_h = sb("edge_h", [P, 2, 2, D])
    same = sb("same", [P, 2, 2, 2 * P])
    masked = sb("masked", [P, 2, 2 * P])
    rows_out = sb("rows_out", [P, 4, 2, RW])
    n_earlier = sb("n_earlier", [P, 2])
    is_dup = sb("is_dup", [P, 2])
    to_dump = sb("to_dump", [P, 2])
    wq_wk = sb("wq_wk", [P, 2, DC, D])
    node_x = wq_wk[:].rearrange("p k c n -> p (k c n)").rearrange("p (s b d) -> p s b d", s=4, b=2)
    node_h = sb("node_h", [P, 2, 2, D])
    node_h2 = sb("node_h2", [P, 2, 2, D])
    node_stats = sb("node_stats", [P, 2, 6])
    node_mv = sb("node_mv", [P, 2, 2, 2])
    affine = sb("affine", [P, 2, 2, 2])
    h_sum = sb("h_sum", [P, 2, D])
    sq_row = sb("sq_row", [1, D])
    sums = sb("sums", [P, 2, DC])
    mean1 = sb("mean1", [P, DC])
    mean_sq = sb("mean_sq", [P, DC])
    var1 = sb("var1", [P, DC])
    shift1 = sb("shift1", [P, DC])
    g1 = sb("g1", [P, DC])
    b1 = sb("b1", [P, DC])
    wq, wk = wq_wk[:, 0], wq_wk[:, 1]
    wv, wo = (sb(n, [P, DC, D])[:] for n in ("wv", "wo"))
    proj = sb("proj", [P, MC, DH])
    x64 = sb("x64", [SEQ, D])
    st64 = sb("st64", [SEQ, 6])
    mv64 = sb("mv64", [SEQ, 2])
    rstd64 = sb("rstd64", [SEQ, 1])
    h64 = sb("h64", [SEQ, D])
    h64T = sb("h64T", [P, DC, SEQ])
    qk = [sb(n, [SEQ, D]) for n in ("q_scaled", "k_scaled")]
    squares = sb("squares", [SEQ, D])
    qkT = [sb(n, [DH, H, SEQ]) for n in ("qT", "kT")]
    v_ones = sb("v_ones", [SEQ, H, DH + 1])
    projT = sb("projT", [DH, M])
    norm2 = [sb(n, [SEQ, H]) for n in ("q_norm2", "k_norm2")]
    peak = [sb(n, [SEQ, H]) for n in ("q_peak", "k_peak")]
    k_peak_all = sb("k_peak_all", [SEQ, H])
    exp_bias = [sb(n, [SEQ, H]) for n in ("q_bias", "k_bias")]
    feat = [sb(n, [SEQ, H, M]) for n in ("q_feat", "k_feat")]
    q_featT = sb("q_featT", [P, H * MC, SEQ])
    kv = sb("kv", [P, H * MC, DH + 1])
    inv_den = sb("inv_den", [SEQ, H])
    attn = sb("attn", [SEQ, D])
    attn_in = sb("attn_in", [P, DC, SEQ])
    attn_full = sb("attn_full", [P, DC, SEQ])

    idx_padded, idx_loaded, idx_float, idx_transposed = map(
        sem, ("idx_padded", "idx_loaded", "idx_float", "idx_transposed"))
    dst_row_loaded, consts, zero_tile, zeroed = map(
        sem, ("dst_row_loaded", "consts", "zero_tile", "zeroed"))
    params_loaded, w_loaded, proj_loaded, x64_loaded = map(
        sem, ("params_loaded", "w_loaded", "proj_loaded", "x64_loaded"))
    h64_ready, h64_transposed, h64T_ready = map(sem, ("h64_ready", "h64_transposed", "h64T_ready"))
    qkv_ready, qk_scaled, qk_transposed, qT_ready, kT_ready, v_ready = map(
        sem, ("qkv_ready", "qk_scaled", "qk_transposed", "qT_ready", "kT_ready", "v_ready"))
    scores_ready, k_peaks, k_peak_ready, bias_ready, exp_done, feat_ready = map(
        sem, ("scores_ready", "k_peaks", "k_peak_ready", "bias_ready", "exp_done", "feat_ready"))
    featT_done, featT_ready, kv_done, kv_ready, attn_done, attn_ready = map(
        sem, ("featT_done", "featT_ready", "kv_done", "kv_ready", "attn_done", "attn_ready"))
    attnT_done, attn_in_ready, wo_done, attention_over = map(
        sem, ("attnT_done", "attn_in_ready", "wo_done", "attention_over"))
    dve_order, pool_order = sem("dve_order"), sem("pool_order")
    slot_filled = sem("slot_filled")
    gathered = [sem(f"gathered{s}") for s in range(4)]
    node_loaded = [sem(f"node_loaded{s}") for s in range(4)]
    scattered = [sem(f"scattered{s}") for s in range(4)]
    var64_ready, rstd64_ready, var_ready, rstd_ready = map(
        sem, ("var64_ready", "rstd64_ready", "var_ready", "rstd_ready"))
    affine_ready, node_h_ready, node_h2_ready, h_added, squares_added = map(
        sem, ("affine_ready", "node_h_ready", "node_h2_ready", "h_added", "squares_added"))
    sq_row_ready, sums_ready = sem("sq_row_ready"), sem("sums_ready")
    edge_var_ready, edge_rstd_ready, edge_affine_ready, edge_h_ready, same_ready, index_ready = map(
        sem, ("edge_var_ready", "edge_rstd_ready", "edge_affine_ready", "edge_h_ready", "same_ready",
              "index_ready"))
    comb_done, rows_ready, dup_ready, dump_ready = map(
        sem, ("comb_done", "rows_ready", "dup_ready", "dump_ready"))

    def steps(eng, step):
        for r in range(4):
            step(0, r, r)
        with eng.Fori(1, FOURS - 1) as q:
            for r in range(4):
                step(q, r, 4 * q + r)
        for r in range(4):
            step(FOURS - 1, r, STEPS - 4 + r)

    def exists(j):
        return not isinstance(j, int) or j < STEPS

    def is_last(j):
        return isinstance(j, int) and j == STEPS - 1

    block = scope.enter_context(nc.Block())

    @block.sync
    def _(sp):
        sp.wait_ge(idx_padded, 2)
        for k, e in enumerate((src, dst)):
            sp.dma_start(edge_rows[0:EF, k, :],
                         e[0:EF * P].rearrange("(t p) -> t p", p=P)).then_inc(idx_loaded, 16)
            sp.dma_start(edge_rows[EF:EF + 1, k, 0:ER],
                         e[EF * P:E].rearrange("(t p) -> t p", t=1)).then_inc(idx_loaded, 16)
        sp.dma_start(x64[:], x[0:SEQ, :]).then_inc(x64_loaded, 16)
        for w, n in ((wq, "Wq"), (wk, "Wk"), (wv, "Wv"), (wo, "Wo")):
            sp.dma_start(w, t["L0_gnn_" + n].rearrange("(c p) n -> p c n", p=P)).then_inc(w_loaded, 16)
        sp.dma_start(proj[:], t["L0_gnn_proj"].rearrange("(c p) d -> p c d", p=P)).then_inc(proj_loaded, 16)
        sp.dma_start(dst_row[:, 0:E], dst.partition_broadcast(P)).then_inc(dst_row_loaded, 16)
        with nc.allow_non_contiguous_dma("512 parameters, feature by partition"):
            sp.dma_start(g1[:], t["L0_gnn_norm1_g"].rearrange("(c p) -> p c", p=P)).then_inc(params_loaded, 16)
            sp.dma_start(b1[:], t["L0_gnn_norm1_b"].rearrange("(c p) -> p c", p=P)).then_inc(params_loaded, 16)
        sp.wait_ge(qkv_ready, 3)
        sp.wait_ge(zero_tile, 1)
        sum_flat = gsum.rearrange("(p t) d -> p (t d)", p=P)

        def load_nodes(q, r, j):
            wait_unless_first(sp, node_h_ready, j - 3)
            wait_unless_first(sp, node_h2_ready, j - 3)
            if is_last(j):
                sp.dma_start(node_x[0:z.REST, r, 0, :], x[z.FULL * P:N, :]).then_inc(node_loaded[r], 16)
            else:
                sp.dma_start(node_x[:, r, :, :],
                             x[bass.ds(j * 2 * P, 2 * P), :].rearrange("(b p) d -> p b d", p=P)
                             ).then_inc(node_loaded[r], 16)
            rows = ZEROED_LAST if is_last(j) else 2
            sp.dma_start(sum_flat[:, bass.ds(j * 2 * RW, rows * RW)], zeros[:, 0:rows * RW]).then_inc(zeroed, 16)

        steps(sp, load_nodes)

    @block.gpsimd
    def _(pool):
        nc.gpsimd.memset(edge_rows[:, 0, :], 0).then_inc(idx_padded, 1)
        nc.gpsimd.memset(edge_rows[:, 1, :], z.PAD).then_inc(idx_padded, 1)
        nc.gpsimd.memset(dst_row[:, E:ET * P], z.PAD).then_inc(consts, 1)
        nc.gpsimd.memset(earlier[:], 1.0).then_inc(pool_order, 1)
        nc.gpsimd.memset(neg_half[:], -0.5).then_inc(pool_order, 1)
        nc.gpsimd.memset(ident[:], 0.0).then_inc(pool_order, 1)
        pool.wait_ge(pool_order, 3)
        nc.gpsimd.affine_select(out=ident[:], in_=ident[:], compare_op=ALU.not_equal, fill=1.0,
                                base=0, pattern=[[-1, P]], channel_multiplier=1).then_inc(consts, 1)
        for b in range(2):
            nc.gpsimd.affine_select(out=earlier[:, b, :], in_=earlier[:, b, :], compare_op=ALU.is_gt,
                                    fill=0.0, base=b * P, pattern=[[-1, 2 * P]],
                                    channel_multiplier=1).then_inc(consts, 1)
        nc.gpsimd.iota(dump_i[:], pattern=[[P, 2]], base=z.DUMP, channel_multiplier=1).then_inc(consts, 1)

        pool.wait_ge(var64_ready, 1)
        nc.gpsimd.tensor_tensor(rstd64[:], rstd64[:], neg_half[0:SEQ, 0:1], ALU.pow).then_inc(rstd64_ready, 1)

        def gather(q, r, j):
            filled, normalised = in_register(pool, j + 1), in_register(pool, j - 3)
            pool.wait_ge(consts, 6)
            pool.wait_ge(slot_filled, filled)
            wait_unless_first(pool, edge_h_ready, normalised)
            for b in range(2):
                nc.gpsimd.indirect_dma_start(
                    edge_x[:, r, b, :], None, x[:, :],
                    bass.IndirectOffsetOnAxis(ap=gather_at[:, r, b:b + 1], axis=0)
                ).then_inc(gathered[r], 16)

        for r in range(3):
            gather(0, r, r)
        pool.wait_ge(k_peaks, 1)
        nc.gpsimd.partition_all_reduce(k_peak_all[:], peak[1][:], SEQ, RMAX).then_inc(k_peak_ready, 1)

        def add_h(s, rows, tiles):
            for b in range(tiles):
                last = nc.gpsimd.tensor_tensor(h_sum[0:rows, b, :], h_sum[0:rows, b, :],
                                               node_h[0:rows, s, b, :], ALU.add)
            last.then_inc(h_added, 1)

        def node_step(q, r, j):
            s = r % 2
            pool.wait_ge(var_ready, j + 1)
            nc.gpsimd.tensor_tensor(affine[:, s, :, 0], affine[:, s, :, 0], neg_half[:, 0:2], ALU.pow
                                    ).then_inc(rstd_ready, 1)
            if not isinstance(j, int) or j > 0:
                pool.wait_ge(node_h_ready, j)
                wait_unless_first(pool, h_added, j - 1)
                add_h(1 - s, P, 2)

        steps(pool, node_step)
        pool.wait_ge(node_h_ready, STEPS)
        pool.wait_ge(h_added, STEPS - 1)
        add_h(1, z.REST, 1)
        pool.wait_ge(var_ready, STEPS + 1)
        nc.gpsimd.tensor_tensor(var1[:], var1[:], neg_half[:], ALU.pow).then_inc(rstd_ready, 1)

        def edge_rstd(j, s):
            pool.wait_ge(edge_var_ready, j + 1)
            nc.gpsimd.tensor_tensor(edge_affine[:, s, :, 0], edge_affine[:, s, :, 0], neg_half[:, 0:2],
                                    ALU.pow).then_inc(edge_rstd_ready, 1)

        def edge_step(q, r, j):
            ready, landed = in_register(pool, j + 1), in_register(pool, 32 * (q + (r > 0)))
            pool.wait_ge(zeroed, ZEROED)
            pool.wait_ge(rows_ready, ready)
            pool.wait_ge(index_ready, ready)
            wait_unless_first(pool, scattered[r - 1], landed)
            for b in range(2):
                nc.gpsimd.indirect_dma_start(
                    gsum[:, :], bass.IndirectOffsetOnAxis(ap=scatter_at[:, r, b:b + 1], axis=0),
                    rows_out[:, r, b, :], None, compute_op=ALU.add).then_inc(scattered[r], 16)
            if exists(j + 3):
                gather(q, (r + 3) % 4, j + 3)
            if exists(j + 2):
                edge_rstd(j + 2, r % 2)

        edge_rstd(0, 0)
        edge_rstd(1, 1)
        steps(pool, edge_step)
        for r in range(4):
            pool.wait_ge(scattered[r], 32 * FOURS)

    @block.scalar
    def _(act):
        act.wait_ge(qkv_ready, 2)
        for k in range(2):
            nc.scalar.activation(qk[k][:], bank[1 + k][0:SEQ, :], ACT.Copy, scale=SCALE).then_inc(qk_scaled, 1)
        act.wait_ge(qk_transposed, 2)
        nc.scalar.activation(qkT[1][:].rearrange("p h n -> p (h n)"), bank[5][0:DH, :], ACT.Copy
                             ).then_inc(kT_ready, 1)
        for k in range(2):
            act.wait_ge(bias_ready, k + 1)
            for h in range(H):
                last = nc.scalar.activation(
                    feat[k][:, h, :], bank[4 * k + h // 2][0:SEQ, h % 2 * M:h % 2 * M + M],
                    ACT.Exp, bias=exp_bias[k][:, h:h + 1])
            last.then_inc(exp_done, 1)

        def square(q, r, j):
            s = r % 2
            act.wait_ge(affine_ready, j + 1)
            wait_unless_first(act, squares_added, j - 1)
            rows, tiles = (z.REST, 1) if is_last(j) else (P, 2)
            for b in range(tiles):
                last = nc.scalar.activation(node_h2[0:rows, s, b, :], node_x[0:rows, r, b, :], ACT.Square,
                                            bias=affine[0:rows, s, b, 1:2], scale=affine[0:rows, s, b, 0:1])
            last.then_inc(node_h2_ready, 1)

        steps(act, square)
        act.wait_ge(squares_added, STEPS)
        nc.scalar.activation(sq_row[:], bank[7][0:1, :], ACT.Copy).then_inc(sq_row_ready, 1)

        def normalise(j, r):
            s = r % 2
            act.wait_ge(edge_affine_ready, j + 1)
            wait_unless_first(act, comb_done, j - 1)
            for b in range(2):
                last = nc.scalar.activation(edge_h[:, s, b, :], edge_x[:, r, b, :], ACT.Identity,
                                            bias=edge_affine[:, s, b, 1:2], scale=edge_affine[:, s, b, 0:1])
            last.then_inc(edge_h_ready, 1)

        normalise(0, 0)

        def edge_step(q, r, j):
            s = r % 2
            if exists(j + 1):
                normalise(j + 1, (r + 1) % 4)
            act.wait_ge(comb_done, j + 1)
            wait_unless_first(act, scattered[r], 32 * q)
            for b in range(2):
                last = nc.scalar.activation(rows_out[:, r, b, 0:D], bank[2 * s + b][:], ACT.Copy)
            last.then_inc(rows_ready, 1)

        steps(act, edge_step)

    @block.vector
    def _(dve):
        o = Order(dve, dve_order)
        nc.vector.memset(zeros[:], 0.0).then_inc(zero_tile, 1)
        nc.vector.memset(ones[:], 1.0).then_inc(consts, 1)
        nc.vector.memset(rows_out[:, :, :, D:RW], 0.0)
        nc.vector.memset(h_sum[:], 0.0)
        nc.vector.memset(v_ones[:], 1.0)
        dve.wait_ge(idx_loaded, 64)
        nc.vector.tensor_copy(edge_rows_f[:], edge_rows[:]).then_inc(idx_float, 1)
        dve.wait_ge(x64_loaded, 16)
        o.then(nc.vector.bn_stats(st64[:], x64[:]))
        o.then(nc.vector.bn_aggr(mv64[:], st64[:]))
        nc.vector.tensor_scalar(rstd64[:], mv64[:, 1:2], LN_EPS, None, ALU.add).then_inc(var64_ready, 1)
        dve.wait_ge(rstd64_ready, 1)
        nc.vector.tensor_scalar(h64[:], x64[:], mv64[:, 0:1], rstd64[:], ALU.subtract, ALU.mult
                                ).then_inc(h64_ready, 1)
        dve.wait_ge(idx_transposed, 2)
        nc.vector.memset(src_col[:, ET:], 0)
        nc.vector.tensor_copy(src_col[:, 0:ET], bank[7][:, 0:ET])
        o.then(nc.vector.tensor_copy(dst_col[:], bank[7][:, ET:2 * ET]))
        for r in range(4):
            nc.vector.tensor_copy(gather_at[:, r, :], src_col[:, 2 * r:2 * r + 2]).then_inc(slot_filled, 1)
        dve.wait_ge(consts, 6)
        o.then(nc.vector.tensor_copy(dump_row[:], dump_i[:]))

        dve.wait_ge(h64_transposed, 2)
        nc.vector.tensor_copy(h64T[:].rearrange("p c n -> p (c n)"), bank[0][:, 0:DC * SEQ])
        nc.vector.tensor_copy(projT[:], bank[6][0:DH, 0:M]).then_inc(h64T_ready, 1)
        dve.wait_ge(qkv_ready, 3)
        nc.vector.tensor_copy(v_ones[:, :, 0:DH], bank[3][0:SEQ, :].rearrange("p (h d) -> p h d", h=H)
                              ).then_inc(v_ready, 1)
        dve.wait_ge(qk_transposed, 1)
        nc.vector.tensor_copy(qkT[0][:].rearrange("p h n -> p (h n)"), bank[4][0:DH, :]).then_inc(qT_ready, 1)
        dve.wait_ge(qk_scaled, 2)
        for k in range(2):
            o.then(nc.vector.tensor_tensor(squares[:], qk[k][:], qk[k][:], ALU.mult))
            o.then(nc.vector.tensor_reduce(norm2[k][:], squares[:].rearrange("p (h d) -> p h d", h=H),
                                           AX_X, ALU.add))
        for k in range(2):
            dve.wait_ge(scores_ready, k + 1)
            for u in range(H // 2):
                last = nc.vector.tensor_reduce(
                    peak[k][:, 2 * u:2 * u + 2],
                    bank[4 * k + u][0:SEQ, :].rearrange("p (h m) -> p h m", h=2), AX_X, ALU.max)
            if k == 1:
                last.then_inc(k_peaks, 1)
                dve.wait_ge(k_peak_ready, 1)
            else:
                o.then(last)
            nc.vector.scalar_tensor_tensor(exp_bias[k][:], norm2[k][:], -0.5,
                                           (k_peak_all if k else peak[0])[:], ALU.mult, ALU.subtract
                                           ).then_inc(bias_ready, 1)
        for k in range(2):
            dve.wait_ge(exp_done, k + 1)
            nc.vector.tensor_scalar(feat[k][:], feat[k][:], float(M) ** -0.5, KEPS, ALU.mult, ALU.add
                                    ).then_inc(feat_ready, 1)
        dve.wait_ge(featT_done, 1)
        for k in range(2):
            last = nc.vector.tensor_copy(q_featT[:, 8 * k:8 * k + 8, :].rearrange("p a n -> p (a n)"),
                                         bank[k][:])
        last.then_inc(featT_ready, 1)
        dve.wait_ge(kv_done, 1)
        for k in range(4):
            last = nc.vector.tensor_copy(kv[:, 4 * k:4 * k + 4, :].rearrange("p a d -> p (a d)"),
                                         bank[4 + k][:, 0:4 * (DH + 1)])
        last.then_inc(kv_ready, 1)
        dve.wait_ge(attn_done, 1)
        for k in range(2):
            heads = bank[2 + k][0:SEQ, 0:4 * (DH + 1)].rearrange("p (h d) -> p h d", h=4)
            inv = inv_den[:, 4 * k:4 * k + 4].rearrange("p (h a) -> p h a", a=1)
            o.then(nc.vector.tensor_scalar(inv, heads[:, :, DH:DH + 1], KEPS, None, ALU.add))
            o.then(nc.vector.reciprocal(inv, inv))
            last = nc.vector.tensor_tensor(
                attn[:, 4 * k * DH:4 * (k + 1) * DH].rearrange("p (h d) -> p h d", h=4),
                heads[:, :, 0:DH], inv.broadcast_to([SEQ, 4, DH]), ALU.mult)
        last.then_inc(attn_ready, 1)
        dve.wait_ge(attnT_done, 1)
        nc.vector.tensor_copy(attn_in[:].rearrange("p c n -> p (c n)"), bank[0][:, 0:DC * SEQ]
                              ).then_inc(attn_in_ready, 1)
        dve.wait_ge(wo_done, 1)
        o.then(nc.vector.tensor_copy(attn_full[:].rearrange("p c n -> p (c n)"), bank[1][:, 0:DC * SEQ]))
        for c in range(DC):
            last = nc.vector.tensor_scalar(attnT[:, c, :], attn_full[:, c, :],
                                           attn_full[:, c, SEQ - 1:SEQ], None, ALU.subtract)
        last.then_inc(attention_over, 1)

        dve.wait_ge(dst_row_loaded, 16)
        NODE_BASE = o.n
        BY_NODE_STEP = 3

        def node_finish(j, r, no):
            s = r % 2
            dve.wait_ge(rstd_ready, j + 1)
            wait_unless_first(dve, h_added, j - 1)
            nc.vector.scalar_tensor_tensor(affine[:, s, :, 1], node_mv[:, s, :, 0], -1.0,
                                           affine[:, s, :, 0], ALU.mult, ALU.mult
                                           ).then_inc(affine_ready, 1)
            rows, tiles = (z.REST, 1) if is_last(j) else (P, 2)
            dve.wait_ge(affine_ready, j + 1)
            for b in range(tiles):
                last = nc.vector.tensor_scalar(node_h[0:rows, s, b, :], node_x[0:rows, r, b, :],
                                               affine[0:rows, s, b, 0:1], affine[0:rows, s, b, 1:2],
                                               ALU.mult, ALU.add)
            last.then_inc(node_h_ready, 1)
            no.count(nc.vector.tensor_copy(node_affine[:, bass.ds(2 * j, 2), :], affine[:, s, :, :]))

        def node_step(q, r, j):
            s = r % 2
            no = Order(dve, dve_order, NODE_BASE + BY_NODE_STEP * j - 1)
            dve.wait_ge(node_loaded[r], 16 * (q + 1))
            for b in range(2):
                last = nc.vector.bn_stats(node_stats[:, b, :], node_x[:, r, b, :])
            if isinstance(j, int) and j == 0:
                no.n = 1
                no.then(last)
            else:
                no.then(last)
                node_finish(j - 1, (r - 1) % 4, no)
            for b in range(2):
                last = nc.vector.bn_aggr(node_mv[:, s, b, :], node_stats[:, b, :])
            no.then(last)
            wait_unless_first(dve, node_h2_ready, j - 1)
            nc.vector.tensor_scalar(affine[:, s, :, 0:1], node_mv[:, s, :, 1:2], LN_EPS, None, ALU.add
                                    ).then_inc(var_ready, 1)
            assert no.n == BY_NODE_STEP

        steps(dve, node_step)
        o = Order(dve, dve_order, NODE_BASE + BY_NODE_STEP * STEPS - 1)
        node_finish(STEPS - 1, 3, o)
        dve.wait_ge(sums_ready, 1)
        o.then(nc.vector.tensor_copy(sums[:].rearrange("p k c -> p (k c)"), bank[6][:, 0:2 * DC]))
        nc.vector.tensor_scalar(mean1[:], sums[:, 0], 1.0 / N, None, ALU.mult)
        o.then(nc.vector.tensor_scalar(var1[:], sums[:, 1], 1.0 / N, None, ALU.mult))
        o.then(nc.vector.tensor_tensor(mean_sq[:], mean1[:], mean1[:], ALU.mult))
        o.then(nc.vector.tensor_tensor(var1[:], var1[:], mean_sq[:], ALU.subtract))
        nc.vector.tensor_scalar(var1[:], var1[:], BN_EPS, None, ALU.add).then_inc(var_ready, 1)
        dve.wait_ge(rstd_ready, STEPS + 1)
        dve.wait_ge(params_loaded, 32)
        o.then(nc.vector.tensor_tensor(bn1[:, 0, :], var1[:], g1[:], ALU.mult))
        o.then(nc.vector.tensor_tensor(shift1[:], mean1[:], bn1[:, 0, :], ALU.mult))
        o.then(nc.vector.tensor_tensor(bn1[:, 1, :], b1[:], shift1[:], ALU.subtract))

        EDGE_BASE = o.base + o.n
        BY_EDGE_STEP = 3

        def edge_statistics(j, r, eo):
            s = r % 2
            dve.wait_ge(gathered[r], 8 * (j - r) + 32)
            for b in range(2):
                last = nc.vector.bn_stats(edge_stats[:, b, :], edge_x[:, r, b, :])
            eo.then(last)
            if exists(j + 4):
                nc.vector.tensor_copy(gather_at[:, r, :], src_col[:, bass.ds(2 * j + 8, 2)]
                                      ).then_inc(slot_filled, 1)
            for b in range(2):
                last = nc.vector.bn_aggr(edge_mv[:, s, b, :], edge_stats[:, b, :])
            eo.then(last)
            wait_unless_first(dve, edge_h_ready, j - 1)
            nc.vector.tensor_scalar(edge_affine[:, s, :, 0], edge_mv[:, s, :, 1], LN_EPS, None, ALU.add
                                    ).then_inc(edge_var_ready, 1)

        def edge_finish(j, s):
            dve.wait_ge(edge_rstd_ready, j + 1)
            nc.vector.scalar_tensor_tensor(edge_affine[:, s, :, 1], edge_mv[:, s, :, 0], -1.0,
                                           edge_affine[:, s, :, 0], ALU.mult, ALU.mult
                                           ).then_inc(edge_affine_ready, 1)

        def rows_with_one_destination(j, r, eo):
            s = r % 2
            wait_unless_first(dve, comb_done, j - 1)
            wait_unless_first(dve, scattered[r], 8 * (j - r))
            for b in range(2):
                last = nc.vector.tensor_scalar(
                    same[:, s, b, :], dst_row[:, bass.ds(j * 2 * P, 2 * P)],
                    dst_col[:, bass.ds(2 * j + b, 1)], None, ALU.is_equal, ALU.add,
                    accum_out=rows_out[:, r, b, D:D + 1])
            last.then_inc(same_ready, 1)
            dve.wait_ge(same_ready, j + 1)
            for b in range(2):
                last = nc.vector.tensor_tensor_reduce(
                    out=masked[:, b, :], in0=same[:, s, b, :], in1=earlier[:, b, :], scale=1.0,
                    scalar=0.0, op0=ALU.mult, op1=ALU.add, accum_out=n_earlier[:, b:b + 1])
            nc.vector.tensor_tensor(to_dump[:], dump_row[:], dst_col[:, bass.ds(2 * j, 2)], ALU.subtract)
            eo.then(last)
            nc.vector.tensor_scalar(is_dup[:], n_earlier[:], 1.0, None, ALU.min).then_inc(dup_ready, 1)
            dve.wait_ge(dup_ready, j + 1)
            nc.vector.tensor_tensor(to_dump[:], to_dump[:], is_dup[:], ALU.mult).then_inc(dump_ready, 1)
            dve.wait_ge(dump_ready, j + 1)
            nc.vector.tensor_tensor(scatter_at[:, r, :], to_dump[:], dst_col[:, bass.ds(2 * j, 2)], ALU.add
                                    ).then_inc(index_ready, 1)

        PRE = Order(dve, dve_order, EDGE_BASE)
        edge_statistics(0, 0, PRE)
        edge_finish(0, 0)
        rows_with_one_destination(0, 0, PRE)
        edge_statistics(1, 1, PRE)
        LOOP_BASE = EDGE_BASE + PRE.n

        def edge_step(q, r, j):
            eo = Order(dve, dve_order, LOOP_BASE + BY_EDGE_STEP * j)
            if exists(j + 1):
                edge_finish(j + 1, (r + 1) % 2)
                rows_with_one_destination(j + 1, (r + 1) % 4, eo)
            if exists(j + 2):
                edge_statistics(j + 2, (r + 2) % 4, eo)
                assert eo.n == BY_EDGE_STEP

        steps(dve, edge_step)

    @block.tensor
    def _(pe):
        pe.wait_ge(consts, 6)
        pe.wait_ge(idx_float, 1)
        for k in range(2):
            nc.tensor.transpose(bank[7][:, k * ET:(k + 1) * ET], edge_rows_f[:, k, :], ident[0:ET, 0:ET]
                                ).then_inc(idx_transposed, 1)
        pe.wait_ge(h64_ready, 1)
        for c in range(DC):
            last = nc.tensor.transpose(bank[0][:, c * SEQ:(c + 1) * SEQ], h64[:, c * P:(c + 1) * P],
                                       ident[0:SEQ, 0:SEQ])
        last.then_inc(h64_transposed, 1)
        pe.wait_ge(proj_loaded, 16)
        for c in range(MC):
            last = nc.tensor.transpose(bank[6][0:DH, c * P:(c + 1) * P], proj[:, c, :], ident[:])
        last.then_inc(h64_transposed, 1)
        pe.wait_ge(h64T_ready, 1)
        pe.wait_ge(w_loaded, 64)
        for k, w in enumerate((wq, wk, wv)):
            for c in range(DC):
                last = nc.tensor.matmul(bank[1 + k][0:SEQ, :], h64T[:, c, :], w[:, c, :],
                                        start=(c == 0), stop=(c == DC - 1))
            last.then_inc(qkv_ready, 1)
        for k in range(2):
            pe.wait_ge(qk_scaled, k + 1)
            for h in range(H):
                last = nc.tensor.transpose(bank[4 + k][0:DH, h * SEQ:(h + 1) * SEQ],
                                           qk[k][:, h * DH:(h + 1) * DH], ident[0:SEQ, 0:SEQ])
            last.then_inc(qk_transposed, 1)
        pe.wait_ge(qT_ready, 1)
        pe.wait_ge(v_ready, 1)
        for k in range(2):
            if k == 1:
                pe.wait_ge(kT_ready, 1)
            for h in range(H):
                last = nc.tensor.matmul(bank[4 * k + h // 2][0:SEQ, h % 2 * M:h % 2 * M + M],
                                        qkT[k][:, h, :], projT[:], start=True, stop=True)
            last.then_inc(scores_ready, 1)
        pe.wait_ge(feat_ready, 1)
        for a in range(H * MC):
            last = nc.tensor.transpose(bank[a // 8][:, a % 8 * SEQ:(a % 8 + 1) * SEQ],
                                       feat[0][:, a // MC, a % MC * P:(a % MC + 1) * P],
                                       ident[0:SEQ, 0:SEQ])
        last.then_inc(featT_done, 1)
        pe.wait_ge(feat_ready, 2)
        for a in range(H * MC):
            last = nc.tensor.matmul(bank[4 + a // 4][:, a % 4 * (DH + 1):(a % 4 + 1) * (DH + 1)],
                                    feat[1][:, a // MC, a % MC * P:(a % MC + 1) * P],
                                    v_ones[:, a // MC, :], start=True, stop=True)
        last.then_inc(kv_done, 1)
        pe.wait_ge(featT_ready, 1)
        pe.wait_ge(kv_ready, 1)
        for h in range(H):
            for m in range(MC):
                last = nc.tensor.matmul(bank[2 + h // 4][0:SEQ, h % 4 * (DH + 1):(h % 4 + 1) * (DH + 1)],
                                        q_featT[:, MC * h + m, :], kv[:, MC * h + m, :],
                                        start=(m == 0), stop=(m == MC - 1))
        last.then_inc(attn_done, 1)
        pe.wait_ge(attn_ready, 1)
        for c in range(DC):
            last = nc.tensor.transpose(bank[0][:, c * SEQ:(c + 1) * SEQ], attn[:, c * P:(c + 1) * P],
                                       ident[0:SEQ, 0:SEQ])
        last.then_inc(attnT_done, 1)
        pe.wait_ge(attn_in_ready, 1)
        for co in range(DC):
            for c in range(DC):
                last = nc.tensor.matmul(bank[1][:, co * SEQ:(co + 1) * SEQ], wo[:, c, co * P:(co + 1) * P],
                                        attn_in[:, c, :], start=(c == 0), stop=(c == DC - 1))
        last.then_inc(wo_done, 1)
        pe.wait_ge(attention_over, 1)

        def add_squares(q, r, j):
            s = r % 2
            pe.wait_ge(node_h2_ready, j + 1)
            rows, tiles = (z.REST, 1) if is_last(j) else (P, 2)
            for b in range(tiles):
                last = nc.tensor.matmul(bank[7][0:1, :], ones[0:rows, :], node_h2[0:rows, s, b, :],
                                        start=(isinstance(j, int) and j == 0 and b == 0), stop=is_last(j),
                                        skip_group_check=True)
            last.then_inc(squares_added, 1)

        steps(pe, add_squares)
        pe.wait_ge(h_added, STEPS)
        for c in range(DC):
            for b in range(2):
                nc.tensor.matmul(bank[6][:, c:c + 1], h_sum[:, b, c * P:(c + 1) * P], ones[:],
                                 start=(b == 0), stop=(b == 1))
        pe.wait_ge(sq_row_ready, 1)
        for c in range(DC):
            last = nc.tensor.matmul(bank[6][:, DC + c:DC + c + 1], sq_row[0:1, c * P:(c + 1) * P],
                                    ones[0:1, :], start=True, stop=True)
        last.then_inc(sums_ready, 1)

        def edge_step(q, r, j):
            s = r % 2
            pe.wait_ge(edge_h_ready, j + 1)
            pe.wait_ge(same_ready, j + 1)
            wait_unless_first(pe, rows_ready, j - 1)
            for b in range(2):
                for a in range(2):
                    last = nc.tensor.matmul(bank[2 * s + b][:], same[:, s, a, b * P:(b + 1) * P],
                                            edge_h[:, s, a, :], start=(a == 0), stop=(a == 1))
            last.then_inc(comb_done, 1)

        steps(pe, edge_step)


def in_pairs(eng, count, step):
    step(0, 0)
    step(1, 1)
    with eng.Fori(1, count // 2 - 2) as k:
        for s in range(2):
            step(2 * k + s, s)
    for i in range(count - 4, count):
        step(i, i % 2)


def group_tiles(z, i):
    if isinstance(i, int) and i == z.NG - 1:
        return [P] * (z.LAST_T - 1) + [z.REST]
    return [P] * z.GT


def next_group(z, i, ahead):
    return not isinstance(i, int) or i + ahead < z.NG


def turns(i, s, by):
    return by // 2 * (i - s) + by


def convolution(nc, scope, z, t, bank, ident, node_affine, attnT, bn1, bn2, gsum, zbuf):
    def sb(name, shape, dt=F32):
        return scope.enter_context(nc.sbuf_tensor(name, shape, dt))

    def sem(name):
        return scope.enter_context(nc.semaphore(name))

    D, DC, GT, GN, NG, SEQ = z.D, z.DC, z.GT, z.GN, z.NG, z.SEQ
    x = t["x"]

    w_conv = sb("w_conv", [P, DC, D])
    w_scaled = sb("w_scaled", [P, DC, D])
    w_high, w_low = sb("w_high", [P, DC, D], F32R), sb("w_low", [P, DC, D], F32R)
    shift_twice = sb("shift_twice", [P, DC, 2])
    bias_high, bias_low = sb("bias_high", [2, D], F32R), sb("bias_low", [2, D], F32R)
    bias_first = sb("bias_first", [2, D])
    bias_rows = sb("bias_rows", [2, D], F32R)
    b_conv = sb("b_conv", [P, DC])
    g2, b2 = sb("g2", [P, DC]), sb("b2", [P, DC])
    sum_in = sb("sum_in", [P, 2, GT, z.RW])
    x_in = sb("x_in", [P, 2, GT, D])
    inv_deg = sb("inv_deg", [P, 2, GT])
    has_edge = sb("has_edge", [P, 2, GT, 2])
    has_edgeT = sb("has_edgeT", [2, 2, GN], F32R)
    mean_in = sb("mean_in", [P, 2, GT, D])
    h = sb("h", [P, 2, GT, D])
    m_high, m_low = sb("m_high", [P, 2, DC, GN], F32R), sb("m_low", [P, 2, DC, GN], F32R)
    relu_out = sb("relu_out", [P, 2, GN])
    zT = sb("zT", [P, 2, DC, GN])
    z_stats = sb("z_stats", [P, DC, NG, 6])
    z_mv = sb("z_mv", [P, DC, 2])
    rstd2 = sb("rstd2", [P, DC])
    neg_half2 = sb("neg_half2", [P, DC])
    shift2 = sb("shift2", [P, DC])

    w_loaded, v_loaded, w_scaled_ready, w_high_ready, w_ready = map(
        sem, ("c_w_loaded", "v_loaded", "w_scaled_ready", "w_high_ready", "w_ready"))
    shift_ready, bias_done, bias_ready = map(sem, ("shift_ready", "bias_done", "c_bias_ready"))
    sum_loaded = [sem(f"sum_loaded{s}") for s in range(2)]
    x_loaded = [sem(f"x_loaded{s}") for s in range(2)]
    z_saved = [sem(f"z_saved{s}") for s in range(2)]
    clamped, inv_ready, has_edge_ready, mean_ready, h_ready = map(
        sem, ("clamped", "inv_ready", "has_edge_ready", "mean_ready", "h_ready"))
    flag_transposed, flag_ready, mT_done, high_ready, low_ready = map(
        sem, ("flag_transposed", "flag_ready", "mT_done", "high_ready", "low_ready"))
    hT_done, conv_done, relu_ready, z_local, z_ready, stats_ready = map(
        sem, ("hT_done", "conv_done", "relu_ready", "z_local", "z_ready", "stats_ready"))
    var2_ready, rstd2_ready, end_order = map(sem, ("var2_ready", "rstd2_ready", "end_order"))

    mT_bank, hT_bank, conv_bank = bank[0:2], bank[2:4], bank[4:6]
    flag_bank, bias_bank = bank[6], bank[7]

    block = scope.enter_context(nc.Block())

    @block.sync
    def _(sp):
        sp.dma_start(w_conv[:], t["L0_gnn_W_conv"].rearrange("(c p) n -> p c n", p=P)).then_inc(w_loaded, 16)
        with nc.allow_non_contiguous_dma("512 parameters, feature by partition"):
            for v, n in ((b_conv, "b_conv"), (g2, "norm2_g"), (b2, "norm2_b")):
                sp.dma_start(v[:], t["L0_gnn_" + n].rearrange("(c p) -> p c", p=P)).then_inc(v_loaded, 16)

        def load(i, s):
            rows = group_tiles(z, i)
            whole = sum(r == P for r in rows)
            wait_unless_first(sp, mean_ready, GT * (i - 1))
            sp.dma_start(sum_in[:, s, 0:len(rows), :],
                         gsum[bass.ds(i * GN, len(rows) * P), :].rearrange("(t p) d -> p t d", p=P)
                         ).then_inc(sum_loaded[s], 16)
            wait_unless_first(sp, h_ready, GT * (i - 1))
            sp.dma_start(x_in[:, s, 0:whole, :],
                         x[bass.ds(i * GN, whole * P), :].rearrange("(t p) d -> p t d", p=P)
                         ).then_inc(x_loaded[s], 16)
            if whole < len(rows):
                sp.dma_start(x_in[0:z.REST, s, whole, :], x[i * GN + whole * P:z.N, :]).then_inc(x_loaded[s], 16)

        def save(i, s):
            width = sum(group_tiles(z, i))
            sp.wait_ge(z_ready, DC * (i + 1))
            sp.dma_start(zbuf[:, bass.ds(i * GN, width)].rearrange("(c p) n -> p c n", p=P),
                         zT[:, s, :, 0:width]).then_inc(z_saved[s], 16)

        def step(i, s):
            if next_group(z, i, 2):
                load(i + 2, s)
            save(i, s)

        load(0, 0)
        load(1, 1)
        in_pairs(sp, NG, step)
        for s in range(2):
            sp.wait_ge(z_saved[s], 16 * (NG // 2))

    @block.gpsimd
    def _(pool):
        nc.gpsimd.memset(neg_half2[:], -0.5).then_inc(var2_ready, 1)
        pool.wait_ge(var2_ready, 2)
        nc.gpsimd.tensor_tensor(rstd2[:], rstd2[:], neg_half2[:], ALU.pow).then_inc(rstd2_ready, 1)

    @block.scalar
    def _(act):
        def mean(i, s, tile, rows):
            if tile == 0:
                act.wait_ge(sum_loaded[s], turns(i, s, 16))
                act.wait_ge(inv_ready, i + 1)
            nc.scalar.activation(mean_in[0:rows, s, tile, :], sum_in[0:rows, s, tile, 0:D], ACT.Copy,
                                 scale=inv_deg[0:rows, s, tile:tile + 1]).then_inc(mean_ready, 1)

        def flags(i, s):
            width = sum(group_tiles(z, i))
            act.wait_ge(flag_transposed, i + 1)
            nc.scalar.activation(has_edgeT[:, s, 0:width], flag_bank[0:2, 0:width], ACT.Copy
                                 ).then_inc(flag_ready, 1)

        def high(i, s, c):
            width = sum(group_tiles(z, i))
            act.wait_ge(mT_done, DC * i + c + 1)
            nc.scalar.activation(m_high[:, s, c, 0:width], mT_bank[c % 2][:, 0:width], ACT.Copy
                                 ).then_inc(high_ready, 1)

        act.wait_ge(w_scaled_ready, 1)
        nc.scalar.activation(w_high[:], w_scaled[:], ACT.Copy).then_inc(w_high_ready, 1)
        act.wait_ge(v_loaded, 48)
        for i in range(2):
            for tile in range(GT):
                mean(i, i, tile, P)
        flags(0, 0)
        for c in range(DC):
            high(0, 0, c)

        def step(i, s):
            width = sum(group_tiles(z, i))
            for c in range(DC):
                act.wait_ge(conv_done, DC * i + c + 1)
                wait_unless_first(act, z_ready, DC * i + c - 1)
                nc.scalar.activation(relu_out[:, c % 2, 0:width], conv_bank[c % 2][:, 0:width], ACT.Relu,
                                     bias=b_conv[:, c:c + 1]).then_inc(relu_ready, 1)
                if next_group(z, i, 1):
                    high(i + 1, 1 - s, c)
                    if c == 1:
                        flags(i + 1, 1 - s)
                if next_group(z, i, 2):
                    rows = group_tiles(z, i + 2)
                    if c < len(rows):
                        mean(i + 2, s, c, rows[c])

        in_pairs(act, NG, step)

    @block.vector
    def _(dve):
        def degrees(i, s):
            nt = len(group_tiles(z, i))
            edges = sum_in[:, s, 0:nt, D:D + 1]
            dve.wait_ge(sum_loaded[s], turns(i, s, 16))
            wait_unless_first(dve, mean_ready, GT * (i - 1))
            wait_unless_first(dve, flag_transposed, i - 1)
            nc.vector.tensor_scalar(inv_deg[:, s, 0:nt].rearrange("p (t a) -> p t a", a=1), edges, 1.0, None,
                                    ALU.max).then_inc(clamped, 1)
            for k in range(2):
                last = nc.vector.tensor_scalar(has_edge[:, s, 0:nt, k:k + 1], edges, 1.0, None, ALU.min)
            last.then_inc(has_edge_ready, 1)
            dve.wait_ge(clamped, i + 1)
            nc.vector.reciprocal(inv_deg[:, s, 0:nt], inv_deg[:, s, 0:nt]).then_inc(inv_ready, 1)

        def layernorm(i, s, tile, rows):
            if tile == 0:
                dve.wait_ge(x_loaded[s], 32 + 16 * (i // 2) if is_last_group(i) else turns(i, s, 16))
            affine = node_affine[0:rows, bass.ds(GT * i + tile, 1), :].rearrange("p a k -> p (a k)")
            nc.vector.tensor_scalar(h[0:rows, s, tile, :], x_in[0:rows, s, tile, :], affine[:, 0:1],
                                    affine[:, 1:2], ALU.mult, ALU.add).then_inc(h_ready, 1)

        def is_last_group(i):
            return isinstance(i, int) and i == NG - 1

        def low(i, s, c):
            width = sum(group_tiles(z, i))
            dve.wait_ge(high_ready, DC * i + c + 1)
            nc.vector.tensor_tensor(m_low[:, s, c, 0:width], mT_bank[c % 2][:, 0:width],
                                    m_high[:, s, c, 0:width], ALU.subtract).then_inc(low_ready, 1)

        dve.wait_ge(w_loaded, 16)
        for c in range(DC):
            for k in range(2):
                nc.vector.tensor_copy(shift_twice[:, c, k:k + 1], bn1[:, 1, c:c + 1])
            last = nc.vector.tensor_scalar(w_scaled[:, c, :], w_conv[:, c, :], bn1[:, 0, c:c + 1], None,
                                           ALU.mult)
        last.then_inc(w_scaled_ready, 1)
        degrees(0, 0)
        degrees(1, 1)
        for tile in range(GT):
            layernorm(0, 0, tile, P)
        dve.wait_ge(w_high_ready, 1)
        nc.vector.tensor_tensor(w_low[:], w_scaled[:], w_high[:], ALU.subtract).then_inc(w_ready, 1)
        dve.wait_ge(bias_done, 1)
        o = Order(dve, end_order)
        o.then(nc.vector.tensor_copy(bias_high[:], bias_bank[0:2, :]))
        nc.vector.tensor_tensor(bias_low[:], bias_bank[0:2, :], bias_high[:], ALU.subtract)
        o.then(nc.vector.tensor_scalar(bias_first[:], bias_high[:], ident[0:2, 0:1], None, ALU.mult))
        nc.vector.scalar_tensor_tensor(bias_rows[:], bias_low[:], ident[0:2, 1:2], bias_first[:],
                                       ALU.mult, ALU.add).then_inc(bias_ready, 1)
        for c in range(DC):
            low(0, 0, c)

        def step(i, s):
            width = sum(group_tiles(z, i))
            wait_unless_first(dve, z_saved[s], 8 * (i - s))
            for c in range(DC):
                dve.wait_ge(relu_ready, DC * i + c + 1)
                dve.wait_ge(hT_done, DC * i + c + 1)
                first = isinstance(i, int) and i == 0
                add = nc.vector.tensor_tensor(zT[:, s, c, 0:width], relu_out[:, c % 2, 0:width],
                                              hT_bank[c % 2][:, 0:width], ALU.add)
                if first:
                    add.then_inc(z_local, 1)
                    dve.wait_ge(z_local, c + 1)
                    add = nc.vector.tensor_tensor(zT[:, s, c, 0:SEQ], zT[:, s, c, 0:SEQ], attnT[:, c, :], ALU.add)
                add.then_inc(z_ready, 1)
                if c == 0 and next_group(z, i, 2):
                    degrees(i + 2, s)
                if next_group(z, i, 1):
                    low(i + 1, 1 - s, c)
                    rows = group_tiles(z, i + 1)
                    if c < len(rows):
                        layernorm(i + 1, 1 - s, c, rows[c])
                dve.wait_ge(z_ready, DC * i + c + 1)
                last = nc.vector.bn_stats(z_stats[:, c, bass.ds(i, 1), :].rearrange("p a k -> p (a k)"),
                                          zT[:, s, c, 0:width])
            last.then_inc(stats_ready, 1)

        in_pairs(dve, NG, step)
        dve.wait_ge(stats_ready, NG)
        for c in range(DC):
            last = nc.vector.bn_aggr(z_mv[:, c, :], z_stats[:, c, :, :].rearrange("p g k -> p (g k)"))
        o.then(last)
        nc.vector.tensor_scalar(rstd2[:].rearrange("p (c a) -> p c a", a=1), z_mv[:, :, 1:2], BN_EPS, None,
                                ALU.add).then_inc(var2_ready, 1)
        dve.wait_ge(rstd2_ready, 1)
        dve.wait_ge(v_loaded, 48)
        o.then(nc.vector.tensor_tensor(bn2[:, 0, :], rstd2[:], g2[:], ALU.mult))
        o.then(nc.vector.tensor_tensor(shift2[:].rearrange("p (c a) -> p c a", a=1), z_mv[:, :, 0:1],
                                       bn2[:, 0, :].rearrange("p (c a) -> p c a", a=1), ALU.mult))
        o.then(nc.vector.tensor_tensor(bn2[:, 1, :], b2[:], shift2[:], ALU.subtract))

    @block.tensor
    def _(pe):
        def flags(i, s):
            rows = group_tiles(z, i)
            pe.wait_ge(has_edge_ready, i + 1)
            wait_unless_first(pe, flag_ready, i)
            for tile, r in enumerate(rows):
                last = nc.tensor.transpose(flag_bank[0:2, tile * P:tile * P + r], has_edge[0:r, s, tile, :],
                                           ident[0:r, 0:r])
            last.then_inc(flag_transposed, 1)

        def transpose(source, s, rows, c, out, done):
            for tile, r in enumerate(rows):
                last = nc.tensor.transpose(out[:, tile * P:tile * P + r], source[0:r, s, tile, c * P:(c + 1) * P],
                                           ident[0:r, 0:r])
            last.then_inc(done, 1)

        def mean_transposes(i, s, c):
            rows = group_tiles(z, i)
            if c == 0:
                pe.wait_ge(mean_ready, z.LAST_T + GT * i if len(rows) < GT else GT * (i + 1))
            wait_unless_first(pe, low_ready, DC * i + c - 1)
            transpose(mean_in, s, rows, c, mT_bank[c % 2], mT_done)

        def h_transposes(i, s, c):
            rows = group_tiles(z, i)
            if c == 0:
                pe.wait_ge(h_ready, z.LAST_T + GT * i if len(rows) < GT else GT * (i + 1))
            wait_unless_first(pe, z_ready, DC * i + c - 1)
            transpose(h, s, rows, c, hT_bank[c % 2], hT_done)

        flags(0, 0)
        pe.wait_ge(w_scaled_ready, 1)
        for c in range(DC):
            last = nc.tensor.matmul(bias_bank[0:2, :], shift_twice[:, c, :], w_conv[:, c, :],
                                    start=(c == 0), stop=(c == DC - 1))
        last.then_inc(bias_done, 1)
        for c in range(DC):
            mean_transposes(0, 0, c)
        pe.wait_ge(w_ready, 1)
        pe.wait_ge(bias_ready, 1)

        def step(i, s):
            width = sum(group_tiles(z, i))
            for c in range(DC):
                h_transposes(i, s, c)
                if c == 0:
                    pe.wait_ge(low_ready, DC * (i + 1))
                    pe.wait_ge(flag_ready, i + 1)
                wait_unless_first(pe, relu_ready, DC * i + c - 1)
                out = conv_bank[c % 2][:, 0:width]
                nc.tensor.matmul(out, bias_rows[:, c * P:(c + 1) * P], has_edgeT[:, s, 0:width],
                                 start=True, stop=False)
                for k in range(DC):
                    for w, m in ((w_high, m_high), (w_high, m_low), (w_low, m_high)):
                        last = nc.tensor.matmul(out, w[:, k, c * P:(c + 1) * P], m[:, s, k, 0:width],
                                                start=False, stop=(k == DC - 1 and w is w_low))
                last.then_inc(conv_done, 1)
                if next_group(z, i, 1):
                    mean_transposes(i + 1, 1 - s, c)
                    if c == 1:
                        flags(i + 1, 1 - s)

        in_pairs(pe, NG, step)


def in_fours(eng, count, step):
    for i in range(4):
        step(i, i)
    with eng.Fori(1, count // 4 - 1) as k:
        for r in range(4):
            step(4 * k + r, r)
    for i in range(count - 4, count):
        step(i, i % 4)


def experts(nc, scope, z, t, bank, ident, bn2, zbuf, out):
    def sb(name, shape, dt=F32):
        return scope.enter_context(nc.sbuf_tensor(name, shape, dt))

    def sem(name):
        return scope.enter_context(nc.semaphore(name))

    D, DC, GT, GN, NG, NE, F, HC = z.D, z.DC, z.GT, z.GN, z.NG, z.NE, z.F, z.HC
    x = t["x"]
    HALF = P // 2
    SH = HC
    CH = HC + 1
    COMB = 32
    assert NG % 4 == 0 and F == HALF and 2 * NE < COMB

    w_in_high, w_in_low = sb("w_in_high", [P, DC, CH * P], F32R), sb("w_in_low", [P, DC, CH * P], F32R)
    w_out_high, w_out_low = sb("w_out_high", [P, CH, D], F32R), sb("w_out_low", [P, CH, D], F32R)
    w_out_scale = sb("w_out_scale", [P, 1])
    b_hidden = sb("b_hidden", [P, CH])
    iota_i, expert_no = sb("iota_i", [P, GT, NE], I32), sb("expert_no", [P, GT, NE])
    pick = [sb(f"pick{k}", [COMB, HC, P]) for k in range(2)]
    pick_expert = sb("pick_expert", [COMB, HC, P], F32R)
    neg_half3 = sb("neg_half3", [P, GT])
    zero3 = sb("zero3", [HALF, D])
    zT_in = sb("zT_in", [P, 2, DC, GN])
    rows = sb("rows", [P, 4, GT, D])
    work = sb("work", [P, (HC + 2) * GN])
    relu_out = work[:, 0:HC * GN].rearrange("p (c n) -> p c n", c=HC)
    product = work[:, HC * GN:].rearrange("p (k n) -> p k n", k=2)
    w_in = rows[:, 2:4].rearrange("p s t d -> p (s t d)")[:, 0:DC * CH * P].rearrange(
        "p (c m) -> p c m", c=DC)
    w_out = work[:, 0:CH * D].rearrange("p (c d) -> p c d", c=CH)
    ln_stats = sb("ln_stats", [P, GT, 6])
    ln_mv = sb("ln_mv", [P, GT, 2])
    ln_rstd, ln_shift = sb("ln_rstd", [P, GT]), sb("ln_shift", [P, GT])
    y = sb("y", [P, GT, D])
    y_high, y_low = sb("y_high", [P, 2, DC, GN], F32R), sb("y_low", [P, 2, DC, GN], F32R)
    logits_T = sb("logits_T", [NE, GN])
    top, top_at = sb("top", [P, GT, 8]), sb("top_at", [P, GT, 8], U32)
    top_no = sb("top_no", [P, GT, 8])
    gap, ratio = sb("gap", [P, GT, 1]), sb("ratio", [P, GT, 1])
    weight = [sb(f"weight{k}", [P, GT, 1]) for k in range(2)]
    chosen = [sb(f"chosen{k}", [P, GT, NE]) for k in range(2)]
    comb = sb("comb", [P, GT, NE])
    comb_high = sb("comb_high", [P, GT, NE], F32R)
    comb_in = sb("comb_in", [P, GT, COMB])
    shared_relu = sb("shared_relu", [P, GN])
    hid_high, hid_low = sb("hid_high", [P, 2, CH, GN], F32R), sb("hid_low", [P, 2, CH, GN], F32R)

    weights_loaded, tables, w_set, w_in_high_ready, w_out_high_ready, weights_ready = map(
        sem, ("e_weights_loaded", "tables", "w_set", "w_in_high_ready", "w_out_high_ready",
              "weights_ready"))
    pool_order3, dve_order3 = sem("pool_order3"), sem("dve_order3")
    x_loaded = [sem(f"x3_loaded{r}") for r in range(4)]
    zT_loaded = [sem(f"zT_loaded{s}") for s in range(2)]
    saved = [sem(f"saved{r}") for r in range(4)]
    bn_ready, bn_transposed, x1_ready, ln_var_ready, ln_rstd_ready, ln_ready, y_ready = map(
        sem, ("bn_ready", "bn_transposed", "x1_ready", "ln_var_ready", "ln_rstd_ready", "ln_ready",
              "y_ready"))
    y_transposed, y_high_ready, y_low_ready = map(sem, ("y_transposed", "y_high_ready", "y_low_ready"))
    gate_done, logits_ready, shared_ready, shared_high, shared_low = map(
        sem, ("gate_done", "logits_ready", "shared_ready", "shared_high", "shared_low"))
    logits_back, gap_ready, ratio_ready, comb_in_ready, comb_transposed, comb_ready = map(
        sem, ("logits_back", "gap_ready", "ratio_ready", "comb_in_ready", "comb_transposed",
              "comb_ready"))
    hidden_done, relu_ready, weights_spread, product_ready, hid_high_ready, hid_low_ready = map(
        sem, ("hidden_done", "hidden_relu_ready", "weights_spread", "product_ready",
              "hid_high_ready", "hid_low_ready"))
    out_done, out_ready = sem("out_done"), sem("out_ready")

    t_bank, hid_bank, out_bank = bank[0:2], bank[2:4], bank[4:6]
    gate_bank, spread_bank = bank[6], bank[7]
    logits_rows = gate_bank[:, 0:GT * NE].rearrange("p (t e) -> p t e", t=GT)

    def count_of(i, tiles):
        return GT * i + tiles

    block = scope.enter_context(nc.Block())

    @block.sync
    def _(sp):
        def load_x(i, r):
            tiles = group_tiles(z, i)
            whole = sum(n == P for n in tiles)
            wait_unless_first(sp, saved[r], 4 * (i - r))
            sp.dma_start(rows[:, r, 0:whole, :],
                         x[bass.ds(i * GN, whole * P), :].rearrange("(t p) d -> p t d", p=P)
                         ).then_inc(x_loaded[r], 16)
            if whole < len(tiles):
                sp.dma_start(rows[0:z.REST, r, whole, :], x[i * GN + whole * P:z.N, :]).then_inc(x_loaded[r], 16)

        def load_z(i, s):
            width = sum(group_tiles(z, i))
            wait_unless_first(sp, bn_transposed, count_of(i - 2, GT))
            sp.dma_start(zT_in[:, s, :, 0:width],
                         zbuf[:, bass.ds(i * GN, width)].rearrange("(c p) n -> p c n", p=P)
                         ).then_inc(zT_loaded[s], 16)

        def store(i, r):
            tiles = group_tiles(z, i)
            whole = sum(n == P for n in tiles)
            sp.wait_ge(out_ready, count_of(i, len(tiles)))
            sp.dma_start(out[bass.ds(i * GN, whole * P), :].rearrange("(t p) d -> p t d", p=P),
                         rows[:, r, 0:whole, :]).then_inc(saved[r], 16)
            if whole < len(tiles):
                sp.dma_start(out[i * GN + whole * P:z.N, :], rows[0:z.REST, r, whole, :]).then_inc(saved[r], 16)

        def step(i, r):
            if isinstance(i, int) and i == 0:
                sp.wait_ge(weights_ready, 1)
            if next_group(z, i, 2):
                load_x(i + 2, (r + 2) % 4)
            if next_group(z, i, 3):
                load_z(i + 3, (r + 1) % 2)
            if not isinstance(i, int) or i > 0:
                store(i - 1, (r - 1) % 4)

        load_z(0, 0)
        load_x(0, 0)
        load_z(1, 1)
        load_x(1, 1)
        sp.wait_ge(w_set, 2)
        for e in range(NE):
            sp.dma_start(w_in[:, :, e * F:(e + 1) * F],
                         t["L0_ffn_W1"][e].rearrange("(c p) f -> p c f", p=P)).then_inc(weights_loaded, 16)
        sp.dma_start(w_in[:, :, SH * P + HALF:CH * P],
                     t["L0_ffn_Ws1"].rearrange("(c p) f -> p c f", p=P)).then_inc(weights_loaded, 16)
        sp.dma_start(w_out[:, 0:HC, :],
                     t["L0_ffn_W2"].rearrange("(c e) f d -> (e f) c d", e=2)).then_inc(weights_loaded, 16)
        for k in range(2):
            sp.dma_start(w_out[k * NE:(k + 1) * NE, SH, :], t["L0_ffn_b2"]).then_inc(weights_loaded, 16)
        sp.dma_start(w_out[2 * NE:2 * NE + 1, SH, :],
                     t["L0_ffn_bs2"].rearrange("(a d) -> a d", a=1)).then_inc(weights_loaded, 16)
        sp.dma_start(w_out[HALF:P, SH, :], t["L0_ffn_Ws2"]).then_inc(weights_loaded, 16)
        with nc.allow_non_contiguous_dma("gate's weights and biases, small"):
            sp.dma_start(w_in[:, :, SH * P:SH * P + NE],
                         t["L0_ffn_Wg"].rearrange("(c p) e -> p c e", p=P)).then_inc(weights_loaded, 16)
            sp.dma_start(b_hidden[:, 0:HC],
                         t["L0_ffn_b1"].rearrange("(c e) f -> (e f) c", e=2)).then_inc(weights_loaded, 16)
            sp.dma_start(b_hidden[0:NE, SH:CH],
                         t["L0_ffn_bg"].rearrange("(p a) -> p a", a=1)).then_inc(weights_loaded, 16)
            sp.dma_start(b_hidden[HALF:P, SH:CH],
                         t["L0_ffn_bs1"].rearrange("(p a) -> p a", a=1)).then_inc(weights_loaded, 16)
        load_z(2, 0)
        in_fours(sp, NG, step)
        store(NG - 1, (NG - 1) % 4)
        for r in range(4):
            sp.wait_ge(saved[r], 16 * (NG // 4) + (16 if r == (NG - 1) % 4 else 0))

    LOADS = NE + 10

    @block.gpsimd
    def _(pool):
        po = Order(pool, pool_order3)
        nc.gpsimd.memset(neg_half3[:], -0.5)
        nc.gpsimd.iota(iota_i[:], pattern=[[0, GT], [1, NE]], base=0, channel_multiplier=0).then_inc(tables, 1)
        po.then(nc.gpsimd.memset(w_out_scale[:], 0.5))
        nc.gpsimd.affine_select(out=w_out_scale[:], in_=w_out_scale[:], compare_op=ALU.is_ge, fill=1.0,
                                base=-2 * NE, pattern=[[0, 1]], channel_multiplier=1).then_inc(tables, 1)
        nc.gpsimd.memset(pick[0][:], 1.0)
        po.then(nc.gpsimd.memset(pick[1][:], 1.0))
        for k in range(2):
            po.then(nc.gpsimd.affine_select(out=pick[k][:], in_=pick[k][:], compare_op=ALU.is_ge, fill=0.0,
                                            base=k * NE * F, pattern=[[P, HC], [1, P]], channel_multiplier=-F))
            last = nc.gpsimd.affine_select(out=pick[k][:], in_=pick[k][:], compare_op=ALU.is_ge, fill=0.0,
                                           base=F - 1 - k * NE * F, pattern=[[-P, HC], [-1, P]],
                                           channel_multiplier=F)
        last.then_inc(tables, 1)

        def rstd(i):
            pool.wait_ge(ln_var_ready, i + 1)
            nt = len(group_tiles(z, i))
            nc.gpsimd.tensor_tensor(ln_rstd[:, 0:nt], ln_rstd[:, 0:nt], neg_half3[:, 0:nt], ALU.pow
                                    ).then_inc(ln_rstd_ready, 1)

        rstd(0)

        def step(i, r):
            s = r % 2
            width = sum(group_tiles(z, i))
            pool.wait_ge(shared_high, i + 1)
            pool.wait_ge(ln_rstd_ready, i + 1)
            wait_unless_first(pool, hid_low_ready, HC * i)
            nc.gpsimd.tensor_tensor(hid_low[HALF:P, s, SH, 0:width], shared_relu[HALF:P, 0:width],
                                    hid_high[HALF:P, s, SH, 0:width], ALU.subtract).then_inc(shared_low, 1)
            pool.wait_ge(shared_low, i + 1)
            if next_group(z, i, 1):
                rstd(i + 1)
            for c in range(HC):
                pool.wait_ge(hid_high_ready, HC * i + c + 1)
                nc.gpsimd.tensor_tensor(hid_low[:, s, c, 0:width], product[:, c % 2, 0:width],
                                        hid_high[:, s, c, 0:width], ALU.subtract).then_inc(hid_low_ready, 1)

        in_fours(pool, NG, step)

    @block.scalar
    def _(act):
        def batch_norm(i, s):
            width = sum(group_tiles(z, i))
            act.wait_ge(zT_loaded[s], turns(i, s, 16))
            for c in range(DC):
                last = nc.scalar.activation(zT_in[:, s, c, 0:width], zT_in[:, s, c, 0:width], ACT.Identity,
                                            bias=bn2[:, 1, c:c + 1], scale=bn2[:, 0, c:c + 1])
            last.then_inc(bn_ready, 1)

        def layernorm(i, r):
            act.wait_ge(ln_ready, i + 1)
            for tile, n in enumerate(group_tiles(z, i)):
                nc.scalar.activation(y[0:n, tile, :], rows[0:n, r, tile, :], ACT.Identity,
                                     bias=ln_shift[0:n, tile:tile + 1], scale=ln_rstd[0:n, tile:tile + 1]
                                     ).then_inc(y_ready, 1)

        def high(i, s, tile):
            tiles = group_tiles(z, i)
            if tile < len(tiles):
                n = tiles[tile]
                act.wait_ge(y_transposed, count_of(i, tile + 1))
                nc.scalar.activation(y_high[:, s, :, tile * P:tile * P + n],
                                     t_bank[tile % 2][:].rearrange("p (c n) -> p c n", c=DC)[:, :, 0:n],
                                     ACT.Copy).then_inc(y_high_ready, 1)

        batch_norm(0, 0)
        act.wait_ge(weights_loaded, 16 * LOADS)
        nc.scalar.activation(w_in_high[:], w_in, ACT.Copy).then_inc(w_in_high_ready, 1)
        batch_norm(1, 1)
        layernorm(0, 0)
        act.wait_ge(w_set, 3)
        nc.scalar.activation(w_out_high[:], w_out, ACT.Copy).then_inc(w_out_high_ready, 1)
        for tile in range(GT):
            high(0, 0, tile)

        def step(i, r):
            s = r % 2
            width = sum(group_tiles(z, i))
            more = next_group(z, i, 1)

            def relu(c):
                act.wait_ge(hidden_done, HC * i + c + 1)
                nc.scalar.activation(relu_out[:, c, 0:width], hid_bank[c % 2][:, 0:width], ACT.Relu,
                                     bias=b_hidden[:, c:c + 1]).then_inc(relu_ready, 1)

            def hidden_high(c):
                act.wait_ge(product_ready, HC * i + c + 1)
                nc.scalar.activation(hid_high[:, s, c, 0:width], product[:, c % 2, 0:width], ACT.Copy
                                     ).then_inc(hid_high_ready, 1)

            act.wait_ge(gate_done, i + 1)
            nc.scalar.activation(logits_T[:, 0:width], gate_bank[0:NE, 0:width], ACT.Identity,
                                 bias=b_hidden[0:NE, SH:CH]).then_inc(logits_ready, 1)
            wait_unless_first(act, shared_low, i)
            nc.scalar.activation(shared_relu[HALF:P, 0:width], gate_bank[HALF:P, 0:width], ACT.Relu,
                                 bias=b_hidden[HALF:P, SH:CH]).then_inc(shared_ready, 1)
            act.wait_ge(shared_ready, i + 1)
            nc.scalar.activation(hid_high[HALF:P, s, SH, 0:width], shared_relu[HALF:P, 0:width], ACT.Copy
                                 ).then_inc(shared_high, 1)
            act.wait_ge(gap_ready, i + 1)
            nt = len(group_tiles(z, i))
            nc.scalar.activation(ratio[:, 0:nt], gap[:, 0:nt], ACT.Exp).then_inc(ratio_ready, 1)
            relu(0)
            if next_group(z, i, 2):
                batch_norm(i + 2, s)
            relu(1)
            act.wait_ge(comb_transposed, i + 1)
            nc.scalar.activation(hid_high[0:COMB, s, SH, 0:width], gate_bank[0:COMB, 0:width], ACT.Copy
                                 ).then_inc(comb_ready, 1)
            if more:
                layernorm(i + 1, (r + 1) % 4)
                high(i + 1, 1 - s, 0)
            hidden_high(0)
            relu(2)
            if more:
                high(i + 1, 1 - s, 1)
            hidden_high(1)
            if more:
                high(i + 1, 1 - s, 2)
            hidden_high(2)
            if more:
                high(i + 1, 1 - s, 3)
            relu(3)
            hidden_high(3)

        in_fours(act, NG, step)

    @block.vector
    def _(dve):
        o = Order(dve, dve_order3)

        def x_plus_norm(i, r, tile):
            tiles = group_tiles(z, i)
            if tile < len(tiles):
                n = tiles[tile]
                if tile == 0:
                    last_group = isinstance(i, int) and i == NG - 1
                    dve.wait_ge(x_loaded[r], 16 * (NG // 4) + 16 if last_group else 4 * (i - r) + 16)
                dve.wait_ge(bn_transposed, count_of(i, tile + 1))
                nc.vector.tensor_tensor(rows[0:n, r, tile, :], rows[0:n, r, tile, :],
                                        t_bank[tile % 2][0:n, :], ALU.add).then_inc(x1_ready, 1)

        def statistics(i, r, tile):
            tiles = group_tiles(z, i)
            if tile < len(tiles):
                n = tiles[tile]
                dve.wait_ge(x1_ready, count_of(i, tile + 1))
                return nc.vector.bn_stats(ln_stats[0:n, tile, :], rows[0:n, r, tile, :])

        def finish_statistics(i, order, last):
            tiles = group_tiles(z, i)
            order.then(last, before=(weights_loaded, 16 * LOADS))
            for tile, n in enumerate(tiles):
                last = nc.vector.bn_aggr(ln_mv[0:n, tile, :], ln_stats[0:n, tile, :])
            order.then(last)
            nt = len(tiles)
            nc.vector.tensor_scalar(ln_rstd[:, 0:nt].rearrange("p (t a) -> p t a", a=1), ln_mv[:, 0:nt, 1:2],
                                    LN_EPS, None, ALU.add).then_inc(ln_var_ready, 1)

        def shift(i):
            nt = len(group_tiles(z, i))
            dve.wait_ge(ln_rstd_ready, i + 1)
            nc.vector.scalar_tensor_tensor(
                ln_shift[:, 0:nt].rearrange("p (t a) -> p t a", a=1), ln_mv[:, 0:nt, 0:1], -1.0,
                ln_rstd[:, 0:nt].rearrange("p (t a) -> p t a", a=1), ALU.mult, ALU.mult).then_inc(ln_ready, 1)

        def low(i, s, tile):
            tiles = group_tiles(z, i)
            if tile < len(tiles):
                n = tiles[tile]
                dve.wait_ge(y_high_ready, count_of(i, tile + 1))
                nc.vector.tensor_tensor(y_low[:, s, :, tile * P:tile * P + n],
                                        t_bank[tile % 2][:].rearrange("p (c n) -> p c n", c=DC)[:, :, 0:n],
                                        y_high[:, s, :, tile * P:tile * P + n], ALU.subtract
                                        ).then_inc(y_low_ready, 1)

        def output(i, r, tile):
            if not isinstance(i, int) or i >= 0:
                tiles = group_tiles(z, i)
                if tile < len(tiles):
                    n = tiles[tile]
                    dve.wait_ge(out_done, count_of(i, tile + 1))
                    nc.vector.tensor_tensor(rows[0:n, r, tile, :], rows[0:n, r, tile, :],
                                            out_bank[tile % 2][0:n, :], ALU.add).then_inc(out_ready, 1)

        nc.vector.memset(w_in[:, :, SH * P:CH * P], 0.0).then_inc(w_set, 1)
        nc.vector.memset(w_out[:, SH, :], 0.0).then_inc(w_set, 1)
        nc.vector.memset(zero3[:], 0.0)
        nc.vector.memset(comb_in[:], 0.0).then_inc(dve_order3, 1)
        o.n = 1
        dve.wait_ge(dve_order3, 1)
        nc.vector.memset(comb_in[:, :, 2 * NE:2 * NE + 1], 1.0)
        for s in range(2):
            nc.vector.tensor_copy(hid_high[0:HALF, s, SH, :], zero3[:])
            nc.vector.tensor_copy(hid_low[0:HALF, s, SH, :], zero3[:])
        dve.wait_ge(tables, 3)
        nc.vector.tensor_copy(expert_no[:], iota_i[:])
        o.then(nc.vector.tensor_tensor(pick_expert[:], pick[0][:], pick[1][:], ALU.add))
        for tile in range(GT):
            x_plus_norm(0, 0, tile)
        dve.wait_ge(weights_loaded, 16 * LOADS)
        nc.vector.tensor_scalar(w_out[:, SH, :], w_out[:, SH, :], w_out_scale[:, 0:1], None, ALU.mult
                                ).then_inc(w_set, 1)
        for tile in range(GT):
            last = statistics(0, 0, tile)
        finish_statistics(0, o, last)
        shift(0)
        dve.wait_ge(w_in_high_ready, 1)
        nc.vector.tensor_tensor(w_in_low[:], w_in, w_in_high[:], ALU.subtract)
        dve.wait_ge(w_out_high_ready, 1)
        nc.vector.tensor_tensor(w_out_low[:], w_out, w_out_high[:], ALU.subtract).then_inc(weights_ready, 1)
        for tile in range(GT):
            low(0, 0, tile)
        BASE = o.n
        BY_STEP = 12

        def step(i, r):
            s = r % 2
            width = sum(group_tiles(z, i))
            nt = len(group_tiles(z, i))
            so = Order(dve, dve_order3, BASE + BY_STEP * i)
            more = next_group(z, i, 1)
            after = (r + 1) % 4

            def weigh(c):
                dve.wait_ge(relu_ready, HC * i + c + 1)
                dve.wait_ge(weights_spread, HC * i + c + 1)
                wait_unless_first(dve, hid_low_ready, HC * i + c - 1)
                nc.vector.tensor_tensor(product[:, c % 2, 0:width], relu_out[:, c, 0:width],
                                        spread_bank[:, 0:width], ALU.mult).then_inc(product_ready, 1)

            if more:
                x_plus_norm(i + 1, after, 0)
            output(i - 1, (r - 1) % 4, 0)
            in_register(dve, i + 1)
            dve.wait_ge(weights_ready, 1)
            dve.wait_ge(logits_back, i + 1)
            for tile in range(nt):
                last = nc.vector.max(top[:, tile, :], logits_rows[:, tile, :])
            so.then(last, before=(weights_ready, 1))
            for tile in range(nt):
                last = nc.vector.max_index(top_at[:, tile, :], top[:, tile, :], logits_rows[:, tile, :])
            nc.vector.tensor_tensor(gap[:, 0:nt], top[:, 0:nt, 1:2], top[:, 0:nt, 0:1], ALU.subtract
                                    ).then_inc(gap_ready, 1)
            so.then(last)
            so.then(nc.vector.tensor_copy(top_no[:, 0:nt], top_at[:, 0:nt]))
            for k in range(2):
                last = nc.vector.tensor_tensor(chosen[k][:, 0:nt], expert_no[:, 0:nt],
                                               top_no[:, 0:nt, k:k + 1].broadcast_to([P, nt, NE]), ALU.is_equal)
            dve.wait_ge(ratio_ready, i + 1)
            so.count(last)
            so.then(nc.vector.tensor_scalar(weight[0][:, 0:nt], ratio[:, 0:nt], 1.0, None, ALU.add))
            so.then(nc.vector.reciprocal(weight[0][:, 0:nt], weight[0][:, 0:nt]))
            so.then(nc.vector.tensor_tensor(weight[1][:, 0:nt], ratio[:, 0:nt], weight[0][:, 0:nt], ALU.mult))
            for k in range(2):
                last = nc.vector.tensor_tensor(chosen[k][:, 0:nt], chosen[k][:, 0:nt],
                                               weight[k][:, 0:nt].broadcast_to([P, nt, NE]), ALU.mult)
            so.then(last)
            so.then(nc.vector.tensor_tensor(comb[:, 0:nt], chosen[0][:, 0:nt], chosen[1][:, 0:nt], ALU.add))
            so.then(nc.vector.tensor_copy(comb_high[:, 0:nt], comb[:, 0:nt]))
            nc.vector.tensor_copy(comb_in[:, 0:nt, 0:NE], comb_high[:, 0:nt])
            nc.vector.tensor_tensor(comb_in[:, 0:nt, NE:2 * NE], comb[:, 0:nt], comb_high[:, 0:nt],
                                    ALU.subtract).then_inc(comb_in_ready, 1)
            if more:
                x_plus_norm(i + 1, after, 1)
                statistics(i + 1, after, 0)
                x_plus_norm(i + 1, after, 2)
                statistics(i + 1, after, 1)
            output(i - 1, (r - 1) % 4, 1)
            if more:
                x_plus_norm(i + 1, after, 3)
                last = statistics(i + 1, after, 2)
                last = statistics(i + 1, after, 3) or last
                finish_statistics(i + 1, so, last)
                shift(i + 1)
            output(i - 1, (r - 1) % 4, 2)
            weigh(0)
            if more:
                low(i + 1, 1 - s, 0)
            weigh(1)
            if more:
                low(i + 1, 1 - s, 1)
            output(i - 1, (r - 1) % 4, 3)
            weigh(2)
            if more:
                low(i + 1, 1 - s, 2)
                low(i + 1, 1 - s, 3)
                assert so.n == BY_STEP, so.n
            weigh(3)

        in_fours(dve, NG, step)
        for tile in range(z.LAST_T):
            output(NG - 1, (NG - 1) % 4, tile)

    @block.tensor
    def _(pe):
        def bn_transposes(i, s, tile):
            tiles = group_tiles(z, i)
            if tile < len(tiles):
                n = tiles[tile]
                if tile == 0:
                    pe.wait_ge(bn_ready, i + 1)
                if tile > 1:
                    pe.wait_ge(x1_ready, count_of(i, tile - 1))
                for c in range(DC):
                    last = nc.tensor.transpose(t_bank[tile % 2][0:n, c * P:(c + 1) * P],
                                               zT_in[:, s, c, tile * P:tile * P + n], ident[:])
                last.then_inc(bn_transposed, 1)

        def y_transposes(i, tile):
            tiles = group_tiles(z, i)
            if tile < len(tiles):
                n = tiles[tile]
                pe.wait_ge(y_ready, count_of(i, tile + 1))
                if tile > 1:
                    pe.wait_ge(y_low_ready, count_of(i, tile - 1))
                for c in range(DC):
                    last = nc.tensor.transpose(t_bank[tile % 2][:, c * P:c * P + n], y[0:n, tile, c * P:(c + 1) * P],
                                               ident[0:n, 0:n])
                last.then_inc(y_transposed, 1)

        def hidden(i, s, c, psum, done):
            width = sum(group_tiles(z, i))
            for k in range(DC):
                for w, m in ((w_in_high, y_high), (w_in_high, y_low), (w_in_low, y_high)):
                    last = nc.tensor.matmul(psum[:, 0:width], w[:, k, c * P:(c + 1) * P], m[:, s, k, 0:width],
                                            start=(k == 0 and m is y_high and w is w_in_high),
                                            stop=(k == DC - 1 and w is w_in_low))
            last.then_inc(done, 1)

        def expert_chunk(i, s, c):
            wait_unless_first(pe, relu_ready, HC * i + c - 1)
            hidden(i, s, c, hid_bank[c % 2], hidden_done)

        def spread(i, s, c):
            width = sum(group_tiles(z, i))
            if c == 0:
                pe.wait_ge(comb_ready, i + 1)
            wait_unless_first(pe, product_ready, HC * i + c)
            nc.tensor.matmul(spread_bank[:, 0:width], pick_expert[:, c, :], hid_high[0:COMB, s, SH, 0:width],
                             start=True, stop=True).then_inc(weights_spread, 1)

        def output(i, s, tile):
            if isinstance(i, int) and i < 0:
                return
            tiles = group_tiles(z, i)
            if tile < len(tiles):
                n = tiles[tile]
                at = slice(tile * P, tile * P + n)
                if tile == 0:
                    pe.wait_ge(shared_low, i + 1)
                    pe.wait_ge(hid_low_ready, HC * (i + 1))
                wait_unless_first(pe, out_ready, count_of(i, tile - 1))
                for k in range(CH):
                    for m, w in ((hid_high, w_out_high), (hid_high, w_out_low), (hid_low, w_out_high)):
                        last = nc.tensor.matmul(out_bank[tile % 2][0:n, :], m[:, s, k, at], w[:, k, :],
                                                start=(k == 0 and m is hid_high and w is w_out_high),
                                                stop=(k == CH - 1 and m is hid_low))
                last.then_inc(out_done, 1)

        for tile in range(GT):
            bn_transposes(0, 0, tile)
        for tile in range(GT):
            y_transposes(0, tile)
        pe.wait_ge(weights_ready, 1)

        def step(i, r):
            s = r % 2
            more = next_group(z, i, 1)
            tiles = group_tiles(z, i)
            pe.wait_ge(y_low_ready, count_of(i, len(tiles)))
            hidden(i, s, SH, gate_bank, gate_done)
            if more:
                bn_transposes(i + 1, 1 - s, 0)
            output(i - 1, 1 - s, 0)
            in_register(pe, i + 1)
            pe.wait_ge(weights_ready, 1)
            pe.wait_ge(logits_ready, i + 1)
            pe.wait_ge(shared_ready, i + 1)
            for tile, n in enumerate(tiles):
                last = nc.tensor.transpose(logits_rows[0:n, tile, :], logits_T[:, tile * P:tile * P + n],
                                           ident[0:NE, 0:NE])
            last.then_inc(logits_back, 1)
            if more:
                bn_transposes(i + 1, 1 - s, 1)
            expert_chunk(i, s, 0)
            if more:
                bn_transposes(i + 1, 1 - s, 2)
            output(i - 1, 1 - s, 1)
            if more:
                bn_transposes(i + 1, 1 - s, 3)
            expert_chunk(i, s, 1)
            pe.wait_ge(comb_in_ready, i + 1)
            for tile, n in enumerate(tiles):
                last = nc.tensor.transpose(gate_bank[0:COMB, tile * P:tile * P + n], comb_in[0:n, tile, :],
                                           ident[0:n, 0:n])
            last.then_inc(comb_transposed, 1)
            output(i - 1, 1 - s, 2)
            spread(i, s, 0)
            if more:
                y_transposes(i + 1, 0)
            expert_chunk(i, s, 2)
            spread(i, s, 1)
            if more:
                y_transposes(i + 1, 1)
            output(i - 1, 1 - s, 3)
            spread(i, s, 2)
            if more:
                y_transposes(i + 1, 2)
                y_transposes(i + 1, 3)
            expert_chunk(i, s, 3)
            spread(i, s, 3)

        in_fours(pe, NG, step)
        for tile in range(z.LAST_T):
            output(NG - 1, (NG - 1) % 2, tile)


_INS = ["x", "src", "dst"] + ["L0_gnn_" + n for n in (
    "norm1_g", "norm1_b", "norm2_g", "norm2_b", "W_conv", "b_conv", "Wq", "Wk", "Wv", "Wo", "proj")] + [
    "L0_ffn_" + n for n in ("Wg", "bg", "W1", "b1", "W2", "b2", "Ws1", "bs1", "Ws2", "bs2")]


def kernel(**inputs):
    import numpy as np
    import concourse.bacc as bacc
    from concourse import mybir as m
    from concourse.bass_utils import run_bass_kernel_spmd as run

    nc = bacc.Bacc("TRN2", target_bir_lowering=False, num_devices=1)
    arrays, args = {}, {}
    for name in _INS:
        a = np.ascontiguousarray(inputs[name])
        arrays[f"in_{name}"] = a
        args[name] = nc.dram_tensor(f"in_{name}", a.shape, m.dt.from_np(a.dtype), kind="ExternalInput").ap()
    shape = arrays["in_x"].shape
    out = nc.dram_tensor("out_0", shape, m.dt.float32, kind="ExternalOutput").ap()
    gnn_moe_kernel(nc, args, out)
    r = run(nc, [arrays], core_ids=[0])
    return r.results[0]["out_0"]
```
